# Optimizing a Trainium2 kernel written in Bass

```python
import numpy as np
import jax
import jax.numpy as jnp

def _softmax(x, axis=-1):
    return jax.nn.softmax(x, axis=axis)

def _gelu(x):
    return jax.nn.gelu(x, approximate=True)

def _silu(x):
    return jax.nn.silu(x)

def _sigmoid(x):
    return jax.nn.sigmoid(x)

def _layernorm(x, axis=-1, eps=1e-05):
    m = jnp.mean(x, axis=axis, keepdims=True)
    v = jnp.var(x, axis=axis, keepdims=True)
    return (x - m) / jnp.sqrt(v + eps)

def _scatter_add(tgt, idx, src, axis=0):
    return tgt.at[idx].add(src)

def _segment_sum(src, seg, n):
    return jax.ops.segment_sum(src, seg, n)
kernel_name = 'mk_gnn_resnorm_d4_gnn_r32_bc7605'

def setup_inputs(seed: int=0):
    np.random.seed(seed)
    _w = jnp.asarray

    def _rec_inputs():
        import jax
        import jax.numpy as jnp
        _gk = jax.random.key(seed)
        x = -0.000202 + 1 * jax.random.normal(jax.random.fold_in(_gk, 1), (3125, 128), jnp.float32)
        _s = jax.random.randint(jax.random.fold_in(_gk, 2), (50000,), 0, 3125, jnp.int32)
        _d = jax.random.randint(jax.random.fold_in(_gk, 3), (50000,), 0, 3125, jnp.int32)
        _loop = jnp.arange(3125, dtype=jnp.int32)
        src = jnp.concatenate([_s, _d, _loop])
        dst = jnp.concatenate([_d, _s, _loop])
        _o = jnp.argsort(dst, stable=True)
        src = src[_o]
        dst = dst[_o]
        edge_attr_64 = 0.000155561 + 1.00019 * jax.random.normal(jax.random.fold_in(_gk, 12), (103125, 64), jnp.float32)
        edge_type_24 = jax.random.randint(jax.random.fold_in(_gk, 14), (103125,), 0, 24, jnp.int32)
        edge_type_8 = jax.random.randint(jax.random.fold_in(_gk, 15), (103125,), 0, 8, jnp.int32)
        edge_weight1 = jax.random.uniform(jax.random.fold_in(_gk, 16), (103125, 1), jnp.float32, 0.0, 0.999998)
        return (x, src, dst, edge_attr_64, edge_type_24, edge_type_8, edge_weight1)
    x, src, dst, edge_attr_64, edge_type_24, edge_type_8, edge_weight1 = _rec_inputs()

    def _L0_gnn_setup():
        import jax, jax.numpy as jnp
        import numpy as np
        N_NODES, N_EDGES = (50000, 18750)
        NODE_DIM, EDGE_DIM = (128, 64)
        H, HD = (4, 32)
        key = jax.random.key(seed)
        k = jax.random.split(key, 6)
        node_features = jax.random.normal(k[0], (N_NODES, NODE_DIM), jnp.float32)
        edge_indices = jax.random.randint(k[1], (2, N_EDGES), 0, N_NODES, jnp.int32)
        edge_features = jax.random.normal(k[2], (N_EDGES, EDGE_DIM), jnp.float32)
        W_node = jax.random.normal(k[3], (H * HD, NODE_DIM), jnp.float32) / np.sqrt(NODE_DIM).astype(np.float32)
        W_edge = jax.random.normal(k[4], (H * HD, EDGE_DIM), jnp.float32) / np.sqrt(EDGE_DIM).astype(np.float32)
        a = jax.random.normal(k[5], (H, 3 * HD), jnp.float32)
        return {'node_features': node_features, 'edge_indices': edge_indices, 'edge_features': edge_features, 'W_node': W_node, 'W_edge': W_edge, 'a': a}
    _L0_gnn_all = _L0_gnn_setup()
    _L0_gnn_in = {k: v for k, v in _L0_gnn_all.items() if k in ('W_node', 'W_edge', 'a')}
    del _L0_gnn_all

    def _L1_gnn_setup():
        import jax, jax.numpy as jnp
        import numpy as np
        N_NODES = 50000
        N_EDGES = 25000
        D_IN = 128
        N_HEAD = 4
        D_OUT = D_IN // N_HEAD
        key = jax.random.key(seed)
        k1, k2, k3, k4, k5 = jax.random.split(key, 5)
        in_feat = jax.random.normal(k1, (N_NODES, D_IN), dtype=jnp.float32)
        edge_ind = jax.random.randint(k2, (2, N_EDGES), 0, N_NODES, dtype=jnp.int64)
        W_proj = jax.random.normal(k3, (D_IN, N_HEAD * D_OUT), dtype=jnp.float32) * (1.0 / np.sqrt(D_IN))
        a_src = jax.random.normal(k4, (1, N_HEAD, D_OUT), dtype=jnp.float32) * (1.0 / np.sqrt(D_OUT))
        a_tgt = jax.random.normal(k5, (1, N_HEAD, D_OUT), dtype=jnp.float32) * (1.0 / np.sqrt(D_OUT))
        bias = jnp.zeros((N_HEAD * D_OUT,), dtype=jnp.float32)
        return {'in_feat': in_feat, 'edge_ind': edge_ind, 'edge_len': N_EDGES, 'W_proj': W_proj, 'a_src': a_src, 'a_tgt': a_tgt, 'bias': bias}
    _L1_gnn_all = _L1_gnn_setup()
    _L1_gnn_in = {k: v for k, v in _L1_gnn_all.items() if k in ('W_proj', 'a_src', 'a_tgt', 'bias')}
    del _L1_gnn_all

    def _L2_gnn_setup():
        import jax, jax.numpy as jnp
        import numpy as np
        N_NODES = 50000
        N_EDGES = 50000
        IN_FEAT = 128
        OUT_FEAT = 128
        NUM_RELS = 8
        key = jax.random.key(seed)
        k_h, k_src, k_dst, k_et, k_nrm, k_w, k_b = jax.random.split(key, 7)
        h = jax.random.normal(k_h, (N_NODES, IN_FEAT), dtype=jnp.float32)
        src = jax.random.randint(k_src, (N_EDGES,), 0, N_NODES, dtype=jnp.int32)
        dst = jax.random.randint(k_dst, (N_EDGES,), 0, N_NODES, dtype=jnp.int32)
        etype = jax.random.randint(k_et, (N_EDGES,), 0, NUM_RELS, dtype=jnp.int32)
        norm = jax.random.uniform(k_nrm, (N_EDGES, 1), dtype=jnp.float32)
        W = jax.random.normal(k_w, (NUM_RELS, IN_FEAT, OUT_FEAT), dtype=jnp.float32)
        b = jax.random.normal(k_b, (NUM_RELS, OUT_FEAT), dtype=jnp.float32)
        return {'h': h, 'src': src, 'dst': dst, 'etype': etype, 'norm': norm, 'W': W, 'b': b}
    _L2_gnn_all = _L2_gnn_setup()
    _L2_gnn_in = {k: v for k, v in _L2_gnn_all.items() if k in ('W', 'b')}
    del _L2_gnn_all

    def _L3_gnn_setup():
        import jax, jax.numpy as jnp
        import numpy as np
        N_NODES = 50000
        N_EDGES = 18750
        N_REL = 24
        CHANNEL = 128
        key = jax.random.key(seed)
        k1, k2, k3, k4 = jax.random.split(key, 4)
        all_emb = jax.random.normal(k1, (N_NODES, CHANNEL), dtype=jnp.float32)
        edge_index = jax.random.randint(k2, (2, N_EDGES), 0, N_NODES, dtype=jnp.int64)
        edge_type = jax.random.randint(k3, (N_EDGES,), 0, N_REL, dtype=jnp.int64)
        weight = jax.random.normal(k4, (N_REL, CHANNEL), dtype=jnp.float32)
        return {'all_emb': all_emb, 'edge_index': edge_index, 'edge_type': edge_type, 'weight': weight}
    _L3_gnn_all = _L3_gnn_setup()
    _L3_gnn_in = {k: v for k, v in _L3_gnn_all.items() if k in ('weight',)}
    del _L3_gnn_all
    return {'x': x, 'src': src, 'dst': dst, 'edge_attr_64': edge_attr_64, 'edge_type_24': edge_type_24, 'edge_type_8': edge_type_8, 'edge_weight1': edge_weight1, 'L0_gnn_W_node': _L0_gnn_in['W_node'], 'L0_gnn_W_edge': _L0_gnn_in['W_edge'], 'L0_gnn_a': _L0_gnn_in['a'], 'L1_gnn_W_proj': _L1_gnn_in['W_proj'], 'L1_gnn_a_src': _L1_gnn_in['a_src'], 'L1_gnn_a_tgt': _L1_gnn_in['a_tgt'], 'L1_gnn_bias': _L1_gnn_in['bias'], 'L2_gnn_W': _L2_gnn_in['W'], 'L2_gnn_b': _L2_gnn_in['b'], 'L3_gnn_weight': _L3_gnn_in['weight']}

def reference(x, src, dst, edge_attr_64, edge_type_24, edge_type_8, edge_weight1, L0_gnn_W_node, L0_gnn_W_edge, L0_gnn_a, L1_gnn_W_proj, L1_gnn_a_src, L1_gnn_a_tgt, L1_gnn_bias, L2_gnn_W, L2_gnn_b, L3_gnn_weight):
    import jax
    import jax.numpy as jnp

    def _L0_gnn_ref(node_features, edge_indices, edge_features, W_node, W_edge, a):
        import jax, jax.numpy as jnp
        import numpy as np
        N_NODES, N_EDGES = (50000, 18750)
        NODE_DIM, EDGE_DIM = (128, 64)
        H, HD = (4, 32)
        num_nodes = node_features.shape[0]
        num_edges = edge_indices.shape[1]
        h = (node_features @ W_node.T).reshape(num_nodes, H, HD)
        e = (edge_features @ W_edge.T).reshape(num_edges, H, HD)
        src, tgt = (edge_indices[0], edge_indices[1])
        h_src = h[src]
        h_tgt = h[tgt]
        att_in = jnp.concatenate([h_src, h_tgt, e], axis=-1)
        att = jnp.sum(att_in * a, axis=-1)
        att = jnp.where(att > 0, att, 0.2 * att)
        m = jnp.maximum(jax.ops.segment_max(att, tgt, num_segments=num_nodes), 0.0)
        ex = jnp.exp(att - m[tgt])
        ones = jnp.ones((num_edges,), node_features.dtype)
        deg = jax.ops.segment_sum(ones, tgt, num_segments=num_nodes)
        denom = jax.ops.segment_sum(ex, tgt, num_segments=num_nodes) + (num_edges - deg)[:, None] * jnp.exp(-m)
        w = ex / denom[tgt]
        h_prime = jax.ops.segment_sum(w[:, :, None] * h_src, tgt, num_segments=num_nodes)
        return h_prime.reshape(num_nodes, H * HD)

    def _L1_gnn_ref(in_feat, edge_ind, edge_len, W_proj, a_src, a_tgt, bias):
        import jax, jax.numpy as jnp
        import numpy as np
        N_NODES = 50000
        N_EDGES = 25000
        D_IN = 128
        N_HEAD = 4
        D_OUT = D_IN // N_HEAD
        n_nodes = in_feat.shape[0]
        n_head, d_out = (a_src.shape[1], a_src.shape[2])
        proj_feat = (in_feat @ W_proj).reshape(n_nodes, n_head, d_out)
        src_score = jnp.sum(proj_feat * a_src, axis=-1)
        tgt_score = jnp.sum(proj_feat * a_tgt, axis=-1)
        src_ind, tgt_ind = (edge_ind[0], edge_ind[1])
        edge_score = jax.nn.leaky_relu(src_score[src_ind] + tgt_score[tgt_ind], negative_slope=0.2)
        edge_score = jnp.exp(edge_score - jnp.max(edge_score))
        neigh_sums = jax.ops.segment_sum(edge_score, tgt_ind, num_segments=n_nodes)
        att_per_edge = edge_score / (neigh_sums[tgt_ind] + 1e-16)
        src_feat_weighted = proj_feat[src_ind] * att_per_edge[..., None]
        out_feat = jax.ops.segment_sum(src_feat_weighted, tgt_ind, num_segments=n_nodes)
        return out_feat.reshape(n_nodes, -1) + bias

    def _L2_gnn_ref(h, src, dst, etype, norm, W, b):
        import jax, jax.numpy as jnp
        import numpy as np
        N_NODES = 50000
        N_EDGES = 50000
        IN_FEAT = 128
        OUT_FEAT = 128
        NUM_RELS = 8
        H = jnp.einsum('ni,rio->rno', h, W)
        msg = (H[etype, src] + b[etype]) * norm
        out = jax.ops.segment_sum(msg, dst, num_segments=h.shape[0])
        return jax.nn.relu(out)

    def _L3_gnn_ref(all_emb, edge_index, edge_type, weight):
        import jax, jax.numpy as jnp
        import numpy as np
        N_NODES = 50000
        N_EDGES = 18750
        N_REL = 24
        CHANNEL = 128
        head, tail = (edge_index[0], edge_index[1])
        edge_relation_emb = weight[edge_type]
        neigh_relation_emb = all_emb[tail] * edge_relation_emb
        res_emb = jax.ops.segment_sum(neigh_relation_emb, head, num_segments=all_emb.shape[0])
        return res_emb
    edge_index = jnp.stack([src, dst])
    x = _layernorm(x + _L0_gnn_ref(x, edge_index, edge_attr_64, L0_gnn_W_node, L0_gnn_W_edge, L0_gnn_a), axis=-1)
    x = _layernorm(x + _L1_gnn_ref(x, edge_index, 103125, L1_gnn_W_proj, L1_gnn_a_src, L1_gnn_a_tgt, L1_gnn_bias), axis=-1)
    x = _layernorm(x + _L2_gnn_ref(x, src, dst, edge_type_8, edge_weight1, L2_gnn_W, L2_gnn_b), axis=-1)
    x = _layernorm(x + _L3_gnn_ref(x, edge_index, edge_type_24, L3_gnn_weight), axis=-1)
    return x

_drawn_inputs = setup_inputs


def setup_inputs(seed=0):
    import zlib

    import numpy as np

    out = dict(_drawn_inputs(seed))
    spreads = {'L1_gnn_bias': (0.0, 0.1)}
    factors = {}
    for name, (base, spread) in spreads.items():
        noise = np.random.default_rng([zlib.crc32(name.encode()), seed]).standard_normal(out[name].shape)
        drawn = base * np.exp(spread * noise) if base else spread * noise
        out[name] = jnp.asarray(drawn.astype(out[name].dtype))
    for name, factor in factors.items():
        out[name] = (out[name] * factor).astype(out[name].dtype)
    return out
```

```python
import concourse.bass as bass
from concourse import mybir
from contextlib import ExitStack


def gnn_resnorm_kernel(
    nc: bass.Bass,
    x: bass.AP,
    src: bass.AP,
    dst: bass.AP,
    edge_attr: bass.AP,
    edge_type_24: bass.AP,
    edge_type_8: bass.AP,
    edge_weight: bass.AP,
    W_node: bass.AP,
    W_edge: bass.AP,
    att_a: bass.AP,
    W_proj: bass.AP,
    att_src: bass.AP,
    att_tgt: bass.AP,
    proj_bias: bass.AP,
    W_rel: bass.AP,
    b_rel: bass.AP,
    rel_weight: bass.AP,
    out: bass.AP,
):
    fp32 = mybir.dt.float32
    bf16 = mybir.dt.bfloat16
    i32 = mybir.dt.int32
    ALU = mybir.AluOpType
    ACT = mybir.ActivationFunctionType
    AX = mybir.AxisListType

    P = 128
    N, D = x.shape
    E = src.shape[0]
    KE = edge_attr.shape[1]
    H = att_a.shape[0]
    HD = D // H
    R8 = W_rel.shape[0]
    R24 = rel_weight.shape[0]
    EPS = 1e-5
    NB = -(-N // P)
    NPAD = NB * P
    NLAST = N - (NB - 1) * P
    HALF = 16
    GT = 4
    GPH = HALF // GT
    T = -(-(-(-(E + NB * (P - 1)) // P)) // (2 * HALF)) * (2 * HALF)
    RINGS = T // (2 * HALF)
    TPAD = -(-T // P) * P
    TG = TPAD // P
    EFULL = E // T
    EREST = E - EFULL * T
    FW = 16
    F_SRC, F_ROW, F_SLO, F_SHI, F_DLOC, F_T24, F_NORM, F_EATT = 0, 1, 2, 3, 4, 5, 6, 8
    MW = D + 1
    RW = D + H
    NS = 2 * H + 1
    VW = D + NS
    HG = HALF * P
    POS_PAD = float(P * 8192 + P - 1)
    ROWS = P * T
    XB = 5
    XI = NB // XB
    assert NB % XB == 0 and (P - 1) * T + 8192 >= ROWS
    HUGE = 1.0e30
    BIG = 2.0 ** 100
    KP = 3 * GT * H

    ctx = ExitStack()
    with ctx:
        ctx.enter_context(nc.allow_non_contiguous_dma(reason="attention vectors laid on partitions"))

        def sb(name, shape, dt=fp32):
            return ctx.enter_context(nc.sbuf_tensor(name, shape, dt))

        sems = {}

        def sem(name):
            if name not in sems:
                sems[name] = ctx.enter_context(nc.semaphore(name))
            return sems[name]

        records = nc.dram_tensor("records", (ROWS, FW), fp32, kind=KIND).ap()
        node_rows = nc.dram_tensor("node_rows", (NPAD, RW), fp32, kind=KIND).ap()
        rel_rows = nc.dram_tensor("rel_rows", (R8 * NPAD, D), fp32, kind=KIND).ap()
        messages = nc.dram_tensor("messages", (ROWS, MW), fp32, kind=KIND).ap()
        edge_rows = nc.dram_tensor("edge_rows", (P, T, RW), fp32, kind=KIND).ap()
        hotT_rows = nc.dram_tensor("hotT_rows", (P, T * P), bf16, kind=KIND).ap()
        blk_rows = nc.dram_tensor("blk_rows", (2, TPAD), i32, kind=KIND).ap()

        rec = sb("rec", [P, T, FW])
        xs = sb("xs", [P, NB, D])
        hbuf = sb("hbuf", [P, T * H])
        h_sb = hbuf[:, 0:NB * D].rearrange("p (b c) -> p b c", c=D)
        rows_sb = hbuf[:, 0:NB * RW].rearrange("p (b c) -> p b c", c=RW)
        att2 = hbuf[:, :].rearrange("p (t h) -> p t h", h=H)
        att = sb("att", [P, T, H])[:, :, :]
        arg_g = sb("arg_g", [P, 2, GT, H])
        pre_g = sb("pre_g", [P, 2, GT, H])
        att_g = sb("att_g", [P, 2, GT * H])
        apart = sb("apart", [P, 2, P], bf16)
        apartT = sb("apartT", [P, 2, P], bf16)
        tab_h = sb("tab_h", [P, 2, HALF, 3, H], bf16)
        far_id = sb("far_id", [P, H, P], bf16)
        ring = sb("ring", [P, 2, HALF, RW])
        idx_ring = sb("idx_ring", [P, 2, HALF], i32)
        row_of = sb("row_of", [P, T], i32)
        blk_dst = sb("blk_dst", [1, TPAD], i32)
        blk_src = sb("blk_src", [1, TPAD], i32)
        oh = sb("oh", [P, 2, 2, GT * P], bf16)
        ohT = sb("ohT", [P, 2, 2, GT * P], bf16)
        ohf = sb("ohf", [P, 2, GT, P])
        scaled = sb("scaled", [P, 2, GT, P])
        iota = sb("iota", [P, P])
        iota_b = sb("iota_b", [P, P], bf16)
        ident = sb("ident", [P, P])
        ident_b = sb("ident_b", [P, P], bf16)
        tri = sb("tri", [P, P])
        ones = sb("ones", [P, P])
        zeros = sb("zeros", [P, 512], bf16)
        tval = sb("tval", [P, TG])
        headmask = sb("headmask", [P, H])
        acol = sb("acol", [P, 5])
        aexp = sb("aexp", [P, 5, H])
        w_nat = sb("w_nat", [P, D])
        we2 = sb("we2", [P, 2 * KE])
        wea2 = sb("wea2", [P, 2, H])
        wpT = sb("wpT", [P, D])
        wx = sb("wx", [P, 2, D + 2 * H])
        w24 = sb("w24", [P, D])
        w24s = sb("w24s", [P, 3, D], bf16)
        bias_bc = sb("bias_bc", [P, D])
        stat = sb("stat", [P, 8, NB * NS])
        tab_f = sb("tab_f", [P, H, NB])
        small = sb("small", [P, 12, 32])
        small_i = sb("small_i", [P, 2, 32], i32)
        blk_w = sb("blk_w", [P, TG, NB - 1])
        blk_i = sb("blk_i", [P, TG], i32)
        TABW = T * 3 * H // 2
        AW = TABW + HG + 3 * T + T * H + 8
        arena = sb("arena", [P, AW])
        raw = arena[:, 0:5 * T].rearrange("p (f t) -> p f t", t=T)
        o = 5 * T
        key = arena[:, o:o + T]
        posf = arena[:, o + T:o + 2 * T]
        msk = arena[:, o + 2 * T:o + 4 * T].rearrange("p (a t) -> p a t", t=T)
        scn = arena[:, o + 4 * T:o + 6 * T].rearrange("p (a t) -> p a t", t=T)
        zrow = arena[:, o + 6 * T:o + 7 * T]
        o += 7 * T
        attr = arena[:, o:o + 2 * HALF * KE].rearrange("p (a w) -> p a w", a=2)
        assert o + 2 * HALF * KE <= AW
        tab_t = arena[:, 0:TABW].bitcast(bf16).rearrange("p (t k h) -> p t k h", k=3, h=H)
        hotT = arena[:, TABW:TABW + HG].bitcast(bf16).rearrange("p (a w) -> p a w", a=2)
        w0 = TABW + HG
        blk_all = arena[:, w0:w0 + T].bitcast(i32)
        same = arena[:, w0 + T:w0 + 2 * T + 1]
        blk_hot = arena[:, w0 + T:w0 + 2 * T]
        back = arena[:, w0 + 2 * T + 8:w0 + 3 * T + 8]
        tab_w = arena[:, w0 + 3 * T + 8:w0 + 3 * T + 8 + T * H].rearrange("p (t h) -> p t h", h=H)

        PS = ctx.enter_context(nc.psum_tensor("PS", [P, 4096], fp32))
        BK = 512

        def bank(i, a=0, b=BK):
            return PS[:, i * BK + a:i * BK + b]

        blk_f = small[:, 4, 0:TG]

        def rec_ring(h):
            return ring[:, h, :, :].rearrange("p t w -> p (t w)")[:, 0:HALF * FW].rearrange("p (t f) -> p t f", f=FW)

        block = ctx.enter_context(nc.Block())

        def loop(eng, n, body):
            body(0, True)
            body(1, False)
            with eng.Fori(2, n) as i:
                body(i, False)

        def ring_steps(eng, body, peel_last=False):
            def step(i, first, *last):
                for h in range(2):
                    for q in range(GPH):
                        body(2 * GPH * i + GPH * h + q, h, q, i, first, *last)
            if peel_last:
                step(0, True, False)
                step(1, False, False)
                with eng.Fori(2, RINGS - 1) as i:
                    step(i, False, False)
                step(RINGS - 1, False, True)
            else:
                loop(eng, RINGS, step)

        def hot4(q):
            return oh[:, q // 2, q % 2, :]

        def before(h, q, k=1):
            j = (GPH * h + q - k) % (2 * GPH)
            return j // GPH, j % GPH

        LASTG = T // GT - 1

        def wait_free(eng, name, value):
            if not (isinstance(value, int) and value <= 0):
                eng.wait_ge(sem(name), value)

        PC = D + 2 * H
        SUM0 = NB * D
        ACC_BANKS = -(-(SUM0 + NB * NS) // BK)
        o = w0 + 3 * T + 8
        vals = arena[:, o:o + GPH * GT * VW].rearrange("p (a t c) -> p a t c", a=GPH, c=VW)
        SW = 3 * GT * VW // 2
        assert SW <= 2 * T and SW <= 2 * GT * P and GPH * GT * VW + SW <= T * H
        parts = [a.bitcast(bf16).rearrange("p (k t c) -> p k t c", k=3, c=VW) for a in (
            arena[:, o + GPH * GT * VW:o + GPH * GT * VW + SW], arena[:, w0 + T:w0 + T + SW],
            ohf[:, :, :, :].rearrange("p a t c -> p (a t c)")[:, 0:SW],
            scaled[:, :, :, :].rearrange("p a t c -> p (a t c)")[:, 0:SW])]
        tab_T = ohf[:, :, :, :].rearrange("p a t c -> p (a t c)")[:, 0:H * P]
        pick = ohT[:, :, :, :].rearrange("p a k c -> p (a k c)").rearrange("p (j c) -> p j c", c=P)
        MID = T // 2
        assert MID <= BK and KP <= P
        w24f = sb("w24f", [P, D])
        x_stage = ohf[:, :, :, :].rearrange("p a t c -> p (a t c)")[:, 0:XB * P]
        xT = scaled[:, :, :, :].rearrange("p a t c -> p (a t c)")[:, 0:XB * P]
        rel_stage = arena[:, 0:XB * R8 * D].rearrange("p (j w) -> p j w", j=XB)
        w_rel = arena[:, o:o + R8 * D].rearrange("p (r c) -> p r c", r=R8)
        b_rel_bc = arena[:, o + R8 * D:o + 2 * R8 * D]
        assert o + 2 * R8 * D <= AW
        xs3 = arena[:, 0:3 * NB * D // 2].bitcast(bf16).rearrange("p (k c) -> p k c", k=3)
        msg_v = messages.rearrange("(p t) w -> p t w", t=T)
        msg_pat = att[:, :, :].rearrange("p t s -> p (t s)")[:, 0:HALF * MW].rearrange("p (t w) -> p t w", w=MW)


        def hold(eng, name, value):
            eng.wait_ge(sem(name), value)
            eng.sem_inc(sem(f"held_{eng_name(eng)}"), 1)

        def eng_name(eng):
            return str(eng.engine).split(".")[-1]

        IN_F = ("src", "dst", "t8", "t24", "w1")

        @block.sync
        def _(sp):
            sp.wait_ge(sem("raw_cleared"), 1)
            for f, a in enumerate((src, dst, edge_type_8, edge_type_24, edge_weight.rearrange("e o -> (e o)"))):
                to = raw[:, f, :] if f == 4 else raw[:, f, :].bitcast(i32)
                sp.dma_start(to[0:EFULL, :], a[0:EFULL * T].rearrange("(p t) -> p t", t=T)).then_inc(sem("raw_loaded"), 16)
                sp.dma_start(to[EFULL:EFULL + 1, 0:EREST], a[EFULL * T:E].rearrange("(o t) -> o t", o=1)).then_inc(sem("raw_loaded"), 16)
            sp.wait_ge(sem("xs_cleared"), 1)
            sp.dma_start(xs[:, 0:NB - 1, :], x[0:(NB - 1) * P, :].rearrange("(b p) c -> p b c", p=P)).then_inc(sem("x_loaded"), 16)
            sp.dma_start(xs[0:NLAST, NB - 1, :], x[(NB - 1) * P:N, :]).then_inc(sem("x_loaded"), 16)
            sp.wait_ge(sem("blk_made"), 1)
            sp.dma_start(blk_rows[0, :].rearrange("(g p) -> p g", p=P), blk_i[:, :]).then_inc(sem("blk_stored"), 16)
            sp.wait_ge(sem("blk_stored"), 16)
            sp.dma_start(blk_dst[:, :], blk_rows[0:1, :]).then_inc(sem("blk_loaded"), 16)

            ea_full = edge_attr[0:EFULL * T, :].rearrange("(p t) k -> p (t k)", t=T)
            ea_rest = edge_attr[EFULL * T:E, :].rearrange("(o t) k -> o (t k)", o=1)
            CW = HALF * KE

            def attr_load(i, first):
                for h in range(2):
                    if not first:
                        sp.wait_ge(sem("attr_transposed"), 4 * i + 2 * h - 2)
                    c = (2 * i + h) * CW
                    sp.dma_start(attr[0:EFULL, h, :], ea_full[:, bass.ds(c, CW)]).then_inc(sem(f"attr_loaded{h}"), 16)
                    n = CW if not isinstance(i, int) or first else min(max(EREST * KE - c, 0), CW)
                    if n:
                        sp.dma_start(attr[EFULL:EFULL + 1, h, 0:n], ea_rest[:, bass.ds(c, n)]).then_inc(sem(f"attr_loaded{h}"), 16)

            whole = EREST // (2 * HALF)
            attr_load(0, True)
            with sp.Fori(1, whole) as i:
                attr_load(i, False)
            for i in range(whole, RINGS):
                attr_load(i, False)
            for h in range(2):
                sp.wait_ge(sem(f"rec_scattered{h}"), 16 * HALF * RINGS)
            sp.dma_start(rec[:, :, :], records.rearrange("(p t) f -> p t f", t=T)).then_inc(sem("rec_loaded"), 16)
            sp.wait_ge(sem("blk_loaded"), 16)
            sp.dma_start(blk_all, blk_rows[0:1, 0:T].to_broadcast([P, T])).then_inc(sem("blk_spread"), 16)
            for L in range(2):
                sp.wait_ge(sem(f"projected{L}"), XI)
                sp.dma_start(node_rows.rearrange("(b p) c -> p b c", p=P), rows_sb).then_inc(sem(f"rows_stored{L}"), 16)

                def save(i, first):
                    for h in range(2):
                        c = bass.ds((2 * i + h) * HG, HG)
                        if L == 1:
                            if not first:
                                sp.wait_ge(sem("looked1"), 2 * GPH * i + GPH * h - GPH)
                            sp.dma_start(hotT[:, h, :], hotT_rows[:, c]).then_inc(sem(f"hotT_loaded1_{h}"), 16)
                        sp.wait_ge(sem(f"gathered{L}_{h}"), 16 * HALF * i + 16 * HALF)
                        sp.dma_start(edge_rows[:, bass.ds((2 * i + h) * HALF, HALF), :], ring[:, h, :, :]).then_inc(sem(f"saved{L}_{h}"), 16)
                        if L == 0:
                            sp.wait_ge(sem("hotT_made"), 2 * GPH * i + GPH * h + GPH)
                            sp.dma_start(hotT_rows[:, c], hotT[:, h, :]).then_inc(sem(f"hotT_saved_{h}"), 16)

                loop(sp, RINGS, save)
                for h in range(2):
                    sp.wait_ge(sem(f"saved{L}_{h}"), 16 * RINGS)
                    if L == 0:
                        sp.wait_ge(sem(f"hotT_saved_{h}"), 16 * RINGS)
                sp.wait_ge(sem(f"scored{L}"), T // GT)

                def reload(i, first):
                    for h in range(2):
                        if L == 0:
                            if not first:
                                sp.wait_ge(sem("looked_m"), 2 * GPH * i + GPH * h - GPH)
                            sp.dma_start(hotT[:, h, :], hotT_rows[:, bass.ds((2 * i + h) * HG, HG)]).then_inc(sem(f"hotT_loaded0_{h}"), 16)
                        if not first:
                            sp.wait_ge(sem(f"weighted{L}"), 2 * GPH * i + GPH * h - GPH)
                        sp.dma_start(ring[:, h, :, :], edge_rows[:, bass.ds((2 * i + h) * HALF, HALF), :]).then_inc(sem(f"rows_loaded{L}_{h}"), 16)

                loop(sp, RINGS, reload)
            rel_v = rel_rows.rearrange("(r b p) c -> p b r c", b=NB, p=P)

            def rel_store(i, first):
                for j in range(XB):
                    sp.wait_ge(sem("rel_made"), XB * i + j + 1)
                    sp.dma_start(rel_v[:, bass.ds(XB * i + j, 1), :, :], rel_stage[:, j, :].rearrange("p (o r c) -> p o r c", o=1, c=D))\
                        .then_inc(sem(f"rel_stored{j}"), 16)

            loop(sp, XI, rel_store)
            sp.wait_ge(sem("blk_made"), 2)
            sp.dma_start(blk_rows[1, :].rearrange("(g p) -> p g", p=P), blk_i[:, :]).then_inc(sem("blk_stored"), 16)
            sp.wait_ge(sem("blk_stored"), 32)
            sp.dma_start(blk_src[:, :], blk_rows[1:2, :]).then_inc(sem("blk_loaded"), 16)
            sp.wait_ge(sem("normed"), 3)

            def load_hots(i, first):
                for h in range(2):
                    if not first:
                        sp.wait_ge(sem("looked_up_g"), 2 * GPH * i + GPH * h - GPH)
                    sp.dma_start(hotT[:, h, :], hotT_rows[:, bass.ds((2 * i + h) * HG, HG)]).then_inc(sem(f"hotT_loaded3_{h}"), 16)

            loop(sp, RINGS, load_hots)
            for h in range(2):
                sp.wait_ge(sem(f"msg_scattered{h}"), 16 * HALF * RINGS)

            def load_messages(i, first):
                for h in range(2):
                    if not first:
                        sp.wait_ge(sem("acc3"), 2 * GPH * i + GPH * h - GPH)
                    sp.dma_start(ring[:, h, :, 0:MW], msg_v[:, bass.ds((2 * i + h) * HALF, HALF), :]).then_inc(sem(f"msg_loaded{h}"), 16)

            loop(sp, RINGS, load_messages)
            sp.wait_ge(sem("normed"), 4)
            sp.dma_start(out[0:(NB - 1) * P, :].rearrange("(b p) c -> p b c", p=P), xs[:, 0:NB - 1, :]).then_inc(sem("out_stored"), 16)
            sp.dma_start(out[(NB - 1) * P:N, :], xs[0:NLAST, NB - 1, :]).then_inc(sem("out_stored"), 16)
            sp.wait_ge(sem("out_stored"), 32)

        @block.gpsimd
        def _(pool):
            pool.memset(arena[:, 0:5 * T].bitcast(i32), 0).then_inc(sem("raw_cleared0"), 1)
            pool.memset(xs[:, :, :], 0.0).then_inc(sem("xs_cleared"), 1)
            pool.memset(attr[:, :, :], 0.0).then_inc(sem("attr_cleared"), 1)
            pool.wait_ge(sem("raw_cleared0"), 1)
            pool.memset(raw[:, 1, :].bitcast(i32), NPAD + P).then_inc(sem("raw_cleared"), 1)
            pool.memset(ring[:, :, :, :], 0.0).then_inc(sem("ring_cleared"), 1)
            pool.memset(ones[:, :], 1.0).then_inc(sem("ones"), 1)
            pool.wait_ge(sem("ring_cleared"), 1)
            pat = ring[:, 0, :, 0:FW]
            pool.memset(ring[:, 0, :, F_DLOC:F_DLOC + 1], -1.0).then_inc(sem("pat_made"), 1)
            pool.iota(iota[:, :], [[1, P]], base=0, channel_multiplier=0, allow_small_or_imprecise_dtypes=True).then_inc(sem("iota"), 1)
            pool.iota(tval[:, :], [[P, TG]], base=0, channel_multiplier=1, allow_small_or_imprecise_dtypes=True).then_inc(sem("iota"), 1)
            pool.wait_ge(sem("ones"), 1)
            pool.affine_select(out=tri[:, :], in_=ones[:, :], compare_op=ALU.is_gt, fill=0.0, base=0,
                               pattern=[[1, P]], channel_multiplier=-1).then_inc(sem("masks"), 1)
            pool.affine_select(out=ident[:, :], in_=ones[:, :], compare_op=ALU.is_equal, fill=0.0, base=0,
                               pattern=[[1, P]], channel_multiplier=-1).then_inc(sem("masks"), 1)
            pool.affine_select(out=headmask[:, :], in_=ones[:, 0:H], compare_op=ALU.is_ge, fill=0.0, base=0,
                               pattern=[[-HD, H]], channel_multiplier=1).then_inc(sem("masks"), 1)
            pool.wait_ge(sem("masks"), 3)
            pool.affine_select(out=headmask[:, :], in_=headmask[:, :], compare_op=ALU.is_ge, fill=0.0, base=HD - 1,
                               pattern=[[HD, H]], channel_multiplier=-1).then_inc(sem("masks"), 1)
            pool.wait_ge(sem("pat_made"), 1)
            steps = T // HALF
            for q in range(steps):
                pool.dma_start(records.rearrange("(p s t) f -> p s t f", p=P, s=steps)[:, q, :, :], pat).then_inc(sem("rec_filled"), 16)
            pool.wait_ge(sem("rec_filled"), 16 * steps)

            last_row = pool.to_reg(ROWS - 1)

            def scatter_records(i, first):
                for h in range(2):
                    hold(pool, "rec_staged", 2 * i + h + 1)
                    for t in range(HALF):
                        pool.indirect_dma_start(
                            out=records[:, :], out_offset=bass.IndirectOffsetOnAxis(ap=idx_ring[:, h, t:t + 1], axis=0),
                            in_=rec_ring(h)[:, t, :], in_offset=None,
                            bounds_check=last_row, oob_is_err=False).then_inc(sem(f"rec_scattered{h}"), 16)

            loop(pool, RINGS, scatter_records)
            def gather(L, table, w, freed):
                def body(i, first):
                    for h in range(2):
                        hold(pool, f"idx_staged{L}", 2 * i + h + 1)
                        if not first:
                            hold(pool, freed, 2 * GPH * i + GPH * h - GPH)
                            if L < 2:
                                hold(pool, f"saved{L}_{h}", 16 * i)
                        for t in range(HALF):
                            pool.indirect_dma_start(
                                out=ring[:, h, t, 0:w], out_offset=None, in_=table,
                                in_offset=bass.IndirectOffsetOnAxis(ap=idx_ring[:, h, t:t + 1], axis=0))\
                                .then_inc(sem(f"gathered{L}_{h}"), 16)
                loop(pool, RINGS, body)

            for L in range(2):
                pool.wait_ge(sem(f"rows_stored{L}"), 16)
                gather(L, node_rows[:, :], RW, f"scored{L}")
            for j in range(XB):
                pool.wait_ge(sem(f"rel_stored{j}"), 16 * XI)
            gather(2, rel_rows[:, :], D, "acc2")

            def scatter_messages(i, first):
                for h in range(2):
                    hold(pool, "msg_made", 2 * GPH * i + GPH * h + GPH)
                    for t in range(HALF):
                        pool.indirect_dma_start(
                            out=messages[:, :], out_offset=bass.IndirectOffsetOnAxis(ap=idx_ring[:, h, t:t + 1], axis=0),
                            in_=ring[:, h, t, 0:MW], in_offset=None,
                            bounds_check=last_row, oob_is_err=False).then_inc(sem(f"msg_scattered{h}"), 16)

            pool.wait_ge(sem("msg_filled"), 16 * (T // HALF))
            loop(pool, RINGS, scatter_messages)

        def rank(dve, tag, key):
            cnt, ntf, incl, base = (small[:, j, 0:NB] for j in range(4))
            before, total = bank(7, 0, NB), bank(7, 32, 32 + NB)
            for b in range(NB):
                if b % 2 == 0:
                    dve.drain()
                nc.vector.tensor_scalar(msk[:, b % 2, :], key, float(b), None, ALU.is_equal, ALU.add,
                                        accum_out=cnt[:, b:b + 1])
            nc.vector.memset(zrow, 0.0)
            nc.vector.memset(posf, POS_PAD).then_inc(sem(f"{tag}_counted"), 1)
            dve.wait_ge(sem(f"{tag}_summed"), 1)
            nc.vector.tensor_scalar(small_i[:, 0, 0:NB], total, float(P - 1), None, ALU.add)
            dve.drain()
            nc.vector.tensor_scalar(small_i[:, 1, 0:NB], small_i[:, 0, 0:NB], 7, None, ALU.logical_shift_right)
            dve.drain()
            nc.vector.tensor_copy(ntf, small_i[:, 1, 0:NB])
            dve.drain()
            nc.vector.tensor_tensor_scan(incl, ntf, zrow[:, 0:NB], 0.0, ALU.add, ALU.add)
            dve.drain()
            nc.vector.tensor_tensor(base, incl, ntf, ALU.subtract)
            nc.vector.tensor_tensor(blk_w[:, :, :], tval[:, :].unsqueeze(2).to_broadcast([P, TG, NB - 1]),
                                    incl[:, 0:NB - 1].unsqueeze(1).to_broadcast([P, TG, NB - 1]), ALU.is_ge)
            dve.drain()
            nc.vector.scalar_tensor_tensor(base, base, float(P), before, ALU.mult, ALU.add)
            nc.vector.tensor_reduce(blk_f, blk_w[:, :, :], AX.X, ALU.add)
            dve.drain()
            nc.vector.tensor_scalar(base, base, -1.0, None, ALU.add)
            nc.vector.tensor_copy(blk_i[:, :], blk_f).then_inc(sem("blk_made"), 1)
            dve.drain()
            mi = msk.bitcast(i32)
            for b in range(NB + 2):
                dve.drain()
                if b < NB:
                    nc.vector.tensor_scalar(mi[:, b % 2, :], key, float(b), None, ALU.is_equal)
                if 1 <= b <= NB:
                    a = b - 1
                    dve.drain()
                    nc.vector.tensor_tensor_scan(scn[:, a % 2, :], mi[:, a % 2, :], zrow, base[:, a:a + 1], ALU.add, ALU.add)
                    dve.drain()
                    nc.vector.copy_predicated(posf, mi[:, a % 2, :], scn[:, a % 2, :])
            dve.drain()
            nc.vector.tensor_copy(mi[:, 0, :], posf)
            dve.drain()
            nc.vector.tensor_scalar(mi[:, 1, :], mi[:, 0, :], P - 1, None, ALU.bitwise_and)
            nc.vector.tensor_scalar(scn[:, 0, :].bitcast(i32), mi[:, 0, :], 7, None, ALU.logical_shift_right)
            dve.drain()
            nc.vector.scalar_tensor_tensor(row_of[:, :], mi[:, 1, :], float(T), scn[:, 0, :].bitcast(i32), ALU.mult, ALU.add)
            dve.drain()

        @block.vector
        def _(dve):
            nc.vector.memset(zeros[:, :], 0.0)
            dve.wait_ge(sem("iota"), 2)
            nc.vector.tensor_copy(iota_b[:, :], iota[:, :])
            dve.wait_ge(sem("masks"), 4)
            nc.vector.tensor_copy(ident_b[:, :], ident[:, :])
            nc.vector.tensor_scalar(far_id[:, :, :], ident[:, :].unsqueeze(1).to_broadcast([P, H, P]), -BIG, None, ALU.mult)
            nc.vector.tensor_tensor(small[:, 6, 0:GT * H], ident[:, 0:GT * H], ident[:, GT * H:2 * GT * H], ALU.add)
            dve.drain()
            nc.vector.tensor_tensor(small[:, 6, 0:GT * H], small[:, 6, 0:GT * H], ident[:, 2 * GT * H:3 * GT * H], ALU.add)
            nc.vector.memset(apart[:, :, :], 0.0)
            dve.drain()
            nc.vector.tensor_copy(pick, small[:, 6, 0:GT * H].unsqueeze(2).to_broadcast([P, GT * H, P]))
            nc.vector.memset(w24[:, :], 0.0).then_inc(sem("w24_cleared"), 1)
            nc.vector.memset(msg_pat, 0.0)
            dve.drain()
            nc.vector.memset(msg_pat[:, :, D:MW], -1.0).then_inc(sem("msg_pat_made"), 1)
            dve.wait_ge(sem("raw_loaded"), 16 * 2 * len(IN_F))
            r = raw.bitcast(i32)
            s_i, d_i, t8_i, t24_i = (r[:, j, :] for j in range(4))
            lo_i, hi_i = msk[:, 0, :].bitcast(i32), msk[:, 1, :].bitcast(i32)
            nc.vector.tensor_copy(rec[:, :, F_SRC], s_i)
            nc.vector.scalar_tensor_tensor(rec[:, :, F_ROW], t8_i, float(NPAD), s_i, ALU.mult, ALU.add)
            nc.vector.tensor_copy(rec[:, :, F_T24], t24_i)
            nc.vector.tensor_copy(rec[:, :, F_NORM], raw[:, 4, :])
            nc.vector.tensor_scalar(lo_i, s_i, P - 1, None, ALU.bitwise_and)
            nc.vector.tensor_scalar(hi_i, s_i, 7, None, ALU.logical_shift_right)
            dve.drain()
            nc.vector.tensor_copy(rec[:, :, F_SLO], lo_i)
            nc.vector.tensor_copy(rec[:, :, F_SHI], hi_i)
            dve.drain()
            nc.vector.tensor_scalar(lo_i, d_i, P - 1, None, ALU.bitwise_and)
            nc.vector.tensor_scalar(hi_i, d_i, 7, None, ALU.logical_shift_right)
            nc.vector.memset(rec[:, :, F_NORM + 1:F_NORM + 2], 0.0)
            dve.drain()
            nc.vector.tensor_copy(rec[:, :, F_DLOC], lo_i)
            nc.vector.tensor_copy(key, hi_i)
            dve.drain()
            rank(dve, "dst", key)

            def stage_records(i, first):
                for h in range(2):
                    k = 2 * i + h
                    if not first:
                        dve.wait_ge(sem(f"rec_scattered{h}"), 16 * HALF * i)
                    elif h == 0:
                        dve.wait_ge(sem("rec_filled"), 16 * (T // HALF))
                    t0 = bass.ds(k * HALF, HALF)
                    nc.vector.tensor_copy(rec_ring(h)[:, :, 0:8], rec[:, t0, 0:8])
                    nc.vector.tensor_copy(idx_ring[:, h, :], row_of[:, t0])
                    dve.wait_ge(sem("eatt_quad"), 2 * k + 2)
                    nc.vector.tensor_copy(rec_ring(h)[:, :, F_EATT:F_EATT + H],
                                          bank(2 + h, 0, HALF * H).rearrange("p (t h) -> p t h", h=H)).then_inc(sem("rec_staged"), 1)

            loop(dve, RINGS, stage_records)

            def split(f, parts):
                for k in range(3):
                    nc.vector.tensor_copy(parts[k], f)
                    dve.drain()
                    if k < 2:
                        nc.vector.tensor_tensor(f, f, parts[k], ALU.subtract)
                        dve.drain()

            def one_hot(n, p, kind, field):
                t0 = bass.ds(n * GT, GT)
                return nc.vector.tensor_tensor(
                    oh[:, p, kind, :].rearrange("p (t c) -> p t c", c=P), iota_b[:, :].unsqueeze(1).to_broadcast([P, GT, P]),
                    rec[:, t0, field:field + 1].to_broadcast([P, GT, P]), ALU.is_equal)

            def groups(last_step, body):
                def step(i, first):
                    for p in range(2):
                        body(2 * i + p, p, first)
                loop(dve, T // GT // 2, step)

            def projected(L):
                def body(i, first):
                    hold(dve, f"proj_mm{L}", i + 1)
                    for c0, nb, bk in ((0, 3, 2), (3, 2, 3)):
                        v = bank(bk, 0, nb * PC).rearrange("p (b c) -> p b c", c=PC)
                        b0 = bass.ds(XB * i + c0, nb)
                        nc.vector.tensor_copy(rows_sb[:, b0, :], v[:, :, 0:RW])
                        last = nc.vector.tensor_copy(tab_f[:, :, :].rearrange("p h b -> p b h")[:, b0, :], v[:, :, RW:RW + H])
                    last.then_inc(sem(f"projected{L}"), 1)
                loop(dve, XI, body)
                dve.wait_ge(sem("blk_spread"), 16)
                nc.vector.tensor_scalar(blk_hot, blk_all, tval[:, 0:1], None, ALU.is_equal).then_inc(sem(f"blk_hot{L}"), 1)
                for j in range(2 * H):
                    dve.wait_ge(sem(f"tab_mm{L}"), j + 1)
                    nc.vector.tensor_copy(tab_w[:, (j % 2) * MID:(j % 2) * MID + MID, j // 2], bank(j, 0, MID))
                dve.drain()
                split(tab_w, [tab_t[:, :, k, :] for k in range(3)])
                nc.vector.memset(small[:, 11, 0:1], 0.0).then_inc(sem("tab_split"), 1)

            def scores(L):
                def term(n, h, q, i, first, early):
                    p = q % 2
                    if q == 0:
                        dve.wait_ge(sem(f"gathered{L}_{h}"), 16 * HALF * i + 16 * HALF)
                    src_terms = ring[:, h, q * GT:q * GT + GT, D:RW]
                    tgt_terms = bank(2 + p, 0, GT * H).rearrange("p (t h) -> p t h", h=H)
                    if L == 1:
                        dve.wait_ge(sem("looked1"), n + 1)
                        nc.vector.tensor_tensor(att[:, bass.ds(n * GT, GT), :], tgt_terms, src_terms, ALU.add).then_inc(sem("scored1"), 1)
                        return
                    nc.vector.tensor_tensor(pre_g[:, p, :, :], rec[:, bass.ds(n * GT, GT), F_EATT:F_EATT + H], src_terms, ALU.add)
                    dve.drain()
                    if not early:
                        dve.wait_ge(sem("att_kept"), n - 1)
                    dve.wait_ge(sem("looked0"), n + 1)
                    nc.vector.tensor_tensor(att_g[:, p, :].rearrange("p (t h) -> p t h", h=H), tgt_terms, pre_g[:, p, :, :], ALU.add)
                    dve.drain()
                    rest = pre_g[:, p, :, :].rearrange("p t h -> p (t h)")
                    W = GT * H
                    for k in range(3):
                        last = nc.vector.tensor_copy(apart[:, p, k * W:k * W + W], att_g[:, p, :] if k == 0 else rest)
                        if k < 2:
                            dve.drain()
                            nc.vector.tensor_tensor(rest, att_g[:, p, :] if k == 0 else rest, apart[:, p, k * W:k * W + W], ALU.subtract)
                            dve.drain()
                    last.then_inc(sem("scored0"), 1)

                def largest(n):
                    for c in range(2):
                        hold(dve, "spread", 2 * n + c + 1)
                        nc.vector.tensor_reduce(att2[:, bass.ds(n * GT + 2 * c, 2), :],
                                                PS[:, (4 + 2 * c) * BK:(6 + 2 * c) * BK].rearrange("p (t h e) -> p t h e", h=H, e=P),
                                                AX.X, ALU.max).then_inc(sem("maxed"), 1)

                def hot(n, q, early):
                    if not early:
                        dve.wait_ge(sem("spread"), 2 * n - 6)
                    nc.vector.tensor_tensor(
                        hot4(q).rearrange("p (t c) -> p t c", c=P), iota_b[:, :].unsqueeze(1).to_broadcast([P, GT, P]),
                        rec[:, bass.ds(n * GT, GT), F_DLOC:F_DLOC + 1].to_broadcast([P, GT, P]), ALU.not_equal).then_inc(sem("hot_made"), 1)

                def body0(n, h, q, i, first, last_pass):
                    start = first and h == 0
                    if not (last_pass and h and q == GPH - 1):
                        hot(n + 1, (q + 1) % GPH, start and q < GPH - 1)
                    if not (start and q == 0):
                        term(n - 1, *before(h, q), i, first, start and q < 3)
                    if not (start and q < 2):
                        largest(n - 2)

                def body1(n, h, q, i, first):
                    term(n, h, q, i, first, False)

                if L == 1:
                    ring_steps(dve, body1)
                else:
                    hot(0, 0, True)
                    ring_steps(dve, body0, peel_last=True)
                    term(LASTG, 1, GPH - 1, RINGS - 1, False, False)
                    largest(LASTG - 1)
                    largest(LASTG)
                    dve.wait_ge(sem("att_kept"), T // GT)
                    maxima()
                dve.drain()
                nc.vector.tensor_scalar(att2[:, :, 0:1], rec[:, :, F_DLOC:F_DLOC + 1], 0.0, -HUGE, ALU.is_lt, ALU.mult)
                nc.vector.scalar_tensor_tensor(att, att, 0.2, att, ALU.mult, ALU.max)
                dve.drain()
                last = nc.vector.tensor_tensor(att, att, att2[:, :, 0:1].to_broadcast([P, T, H]), ALU.add)
                dve.drain()

            def maxima():
                nc.vector.memset(same[:, 0:1], 0.0)
                nc.vector.memset(same[:, T:T + 1], 0.0)
                nc.vector.tensor_tensor(same[:, 1:T], blk_all[:, 1:T], blk_all[:, 0:T - 1], ALU.is_equal)
                dve.drain()
                for h in range(H):
                    nc.vector.tensor_tensor_scan(back[:, ::-1], same[:, T:0:-1], att2[:, ::-1, h], 0.0, ALU.mult, ALU.max)
                    nc.vector.tensor_tensor_scan(tab_w[:, :, h], same[:, 0:T], att2[:, :, h], 0.0, ALU.mult, ALU.max)
                    dve.drain()
                    nc.vector.tensor_tensor(tab_w[:, :, h], tab_w[:, :, h], back, ALU.max)
                    dve.drain()
                dve.drain()
                split(tab_w, [tab_t[:, :, k, :] for k in range(3)])
                for a in parts:
                    nc.vector.memset(a[:, 0, :, VW - 1:VW], 1.0)
                nc.vector.memset(small[:, 11, 2:3], 0.0).then_inc(sem("tab_split"), 1)

            def global_max():
                nc.vector.tensor_reduce(small[:, 5, 0:1], att, AX.XY, ALU.max).then_inc(sem("lane_max"), 1)
                dve.wait_ge(sem("lane_max_turned"), 1)
                nc.vector.tensor_reduce(small[0:1, 5, 1:2], bank(7, 0, P)[0:1, :], AX.X, ALU.max).then_inc(sem("one_max"), 1)
                dve.wait_ge(sem("max_spread"), 1)
                nc.vector.tensor_scalar(small[:, 5, 2:3], bank(7, P, P + 1), -1.0, None, ALU.mult).then_inc(sem("max_ready"), 1)

            def weigh(L):
                w = D + (2 * H if L == 0 else H)

                def scale(n, h, q, i):
                    if q == 0:
                        dve.wait_ge(sem(f"rows_loaded{L}_{h}"), 16 * i + 16)
                    dve.wait_ge(sem(f"weights_made{L}"), n + 1)
                    nc.vector.tensor_tensor(
                        vals[:, q, :, 0:D].rearrange("p t (h c) -> p t h c", h=H),
                        ring[:, h, q * GT:q * GT + GT, 0:D].rearrange("p t (h c) -> p t h c", h=H),
                        vals[:, q, :, D:D + H].unsqueeze(3).to_broadcast([P, GT, H, HD]), ALU.mult).then_inc(sem(f"weighted{L}"), 1)

                def rest(n, q):
                    dve.wait_ge(sem(f"part0_{L}"), n + 1)
                    nc.vector.tensor_tensor(vals[:, q, :, 0:w], vals[:, q, :, 0:w], parts[q][:, 0, :, 0:w], ALU.subtract).then_inc(sem(f"rest{L}"), 1)

                def last_part(n, q, early):
                    dve.wait_ge(sem(f"part1_{L}"), n + 1)
                    nc.vector.tensor_tensor(parts[q][:, 2, :, 0:w], vals[:, q, :, 0:w], parts[q][:, 1, :, 0:w], ALU.subtract)
                    if not early:
                        dve.wait_ge(sem(f"acc{L}"), n - 3)
                    nc.vector.tensor_tensor(
                        hot4(q).rearrange("p (t c) -> p t c", c=P), iota_b[:, :].unsqueeze(1).to_broadcast([P, GT, P]),
                        rec[:, bass.ds(n * GT, GT), F_DLOC:F_DLOC + 1].to_broadcast([P, GT, P]), ALU.is_equal).then_inc(sem(f"parts_made{L}"), 1)

                def body(n, h, q, i, first):
                    start = first and h == 0
                    if L == 0:
                        dve.wait_ge(sem("looked_m"), n + 1)
                        nc.vector.tensor_tensor(arg_g[:, q % 2, :, :], att[:, bass.ds(n * GT, GT), :],
                                                bank(7, 0, GT * H).rearrange("p (t h) -> p t h", h=H),
                                                ALU.subtract).then_inc(sem("shifted"), 1)
                    if not (start and q < 1):
                        scale(n - 1, *before(h, q), i)
                    if not (start and q < 2):
                        rest(n - 2, before(h, q, 2)[1])
                    if not (start and q < 3):
                        last_part(n - 3, before(h, q, 3)[1], first and GPH * h + q < 7)

                def weigh_norms(n, h, q, i, first):
                    if not (first and h == 0 and q < 2):
                        dve.wait_ge(sem("acc2"), n - 1)
                    for t in range(GT):
                        e = bass.ds(n * GT + t, 1)
                        last = nc.vector.tensor_scalar(ohf[:, q % 2, t, :], iota[:, :], rec[:, e, F_DLOC],
                                                       rec[:, e, F_NORM], ALU.is_equal, ALU.mult)
                    last.then_inc(sem("weighted2"), 1)

                if L == 2:
                    ring_steps(dve, weigh_norms)
                    return
                ring_steps(dve, body)
                scale(LASTG, 1, GPH - 1, RINGS - 1)
                rest(LASTG - 1, GPH - 2)
                last_part(LASTG - 2, GPH - 3, False)
                rest(LASTG, GPH - 1)
                last_part(LASTG - 1, GPH - 2, False)
                last_part(LASTG, GPH - 1, False)

            def norm(L):
                acc = PS[:, 0:NB * D]
                acc3 = acc.rearrange("p (b c) -> p b c", c=D)
                y = h_sb
                dve.wait_ge(sem(f"acc{L}"), T // GT)
                if L < 2:
                    sums, den, edg = stat[:, 0, :], stat[:, 1, 0:NB * H], stat[:, 6, 0:NB]
                    s3 = sums.rearrange("p (b s) -> p b s", s=NS)
                    d3 = den.rearrange("p (b h) -> p b h", h=H)
                    nc.vector.tensor_copy(sums, PS[:, SUM0:SUM0 + NB * NS])
                    dve.drain()
                    if L == 0:
                        has = stat[:, 3, 0:NB]
                        nc.vector.tensor_scalar(edg, s3[:, :, NS - 1], -1.0, float(E), ALU.mult, ALU.add)
                        nc.vector.tensor_scalar(has, s3[:, :, NS - 1], 1.0, None, ALU.max)
                        dve.drain()
                        nc.vector.reciprocal(has, has)
                        dve.drain()
                        nc.vector.tensor_tensor(edg, edg, has, ALU.mult)
                        dve.drain()
                        nc.vector.tensor_tensor(d3, s3[:, :, H:2 * H], edg.unsqueeze(2).to_broadcast([P, NB, H]), ALU.mult)
                        nc.vector.tensor_scalar(has, s3[:, :, NS - 1], 0.0, None, ALU.is_equal)
                        dve.drain()
                        nc.vector.tensor_tensor(d3, d3, s3[:, :, 0:H], ALU.add)
                        dve.drain()
                        nc.vector.tensor_tensor(d3, d3, has.unsqueeze(2).to_broadcast([P, NB, H]), ALU.add)
                    else:
                        nc.vector.tensor_scalar(d3, s3[:, :, 0:H], 1e-16, None, ALU.add)
                    dve.drain()
                    nc.vector.reciprocal(den, den)
                    dve.drain()
                    nc.vector.tensor_tensor(y.rearrange("p b (h c) -> p (b h) c", h=H), acc.rearrange("p (g c) -> p g c", c=HD),
                                            den.unsqueeze(2).to_broadcast([P, NB * H, HD]), ALU.mult)
                    dve.drain()
                    nc.vector.tensor_tensor(y, y, xs[:, :, :], ALU.add)
                    dve.drain()
                    if L == 1:
                        nc.vector.tensor_tensor(y, y, bias_bc[:, :].unsqueeze(1).to_broadcast([P, NB, D]), ALU.add)
                        dve.drain()
                elif L == 2:
                    nc.vector.scalar_tensor_tensor(y, acc3, 0.0, xs[:, :, :], ALU.max, ALU.add)
                    dve.drain()
                else:
                    nc.vector.tensor_tensor(y, acc3, xs[:, :, :], ALU.add)
                    dve.drain()
                tot, var = stat[:, 4, 0:NB], stat[:, 5, 0:NB]
                nc.vector.tensor_reduce(tot, y, AX.X, ALU.add)
                dve.drain()
                nc.vector.tensor_scalar(tot, tot, 1.0 / D, None, ALU.mult)
                dve.drain()
                nc.vector.tensor_tensor(y, y, tot.unsqueeze(2).to_broadcast([P, NB, D]), ALU.subtract)
                dve.drain()
                sq = arena[:, 0:NB * D].rearrange("p (b c) -> p b c", c=D)
                nc.vector.tensor_tensor(sq, y, y, ALU.mult)
                dve.drain()
                nc.vector.tensor_reduce(var, sq, AX.X, ALU.add)
                dve.drain()
                nc.vector.tensor_scalar(var, var, 1.0 / D, EPS, ALU.mult, ALU.add).then_inc(sem("var_made"), 1)
                dve.wait_ge(sem("std_made"), L + 1)
                nc.vector.reciprocal(stat[:, 7, 0:NB], stat[:, 6, 0:NB])
                dve.drain()
                nc.vector.tensor_tensor(xs[:, :, :], y, stat[:, 7, 0:NB].unsqueeze(2).to_broadcast([P, NB, D]), ALU.mult).then_inc(sem("normed"), 1)
                dve.drain()

            def relations():
                def body(i, first):
                    for j in range(XB):
                        n = XB * i + j
                        dve.wait_ge(sem("rel_mm"), n + 1)
                        if not first:
                            dve.wait_ge(sem(f"rel_stored{j}"), 16 * i)
                        nc.vector.tensor_tensor(rel_stage[:, j, :], PS[:, (2 + 2 * (j % 3)) * BK:(4 + 2 * (j % 3)) * BK],
                                                b_rel_bc, ALU.add).then_inc(sem("rel_made"), 1)
                dve.wait_ge(sem("rel_loaded"), 32)
                loop(dve, XI, body)

            def make_messages():
                def product(i, h, q):
                    n, p = 2 * GPH * i + GPH * h + q, q % 2
                    t0 = bass.ds(n * GT, GT)
                    dve.wait_ge(sem("rel_copied"), n + 1)
                    nc.vector.tensor_tensor(ring[:, h, q * GT:q * GT + GT, 0:D], bank(2 + p).rearrange("p (t c) -> p t c", c=D),
                                            scaled[:, p, :, :], ALU.mult)
                    nc.vector.tensor_copy(ring[:, h, q * GT:q * GT + GT, D:MW], rec[:, t0, F_SLO:F_SLO + 1]).then_inc(sem("msg_made"), 1)

                def hot(n, q, early):
                    if not early:
                        dve.wait_ge(sem("transposed_g"), n - 3)
                    nc.vector.tensor_tensor(
                        hot4(q).rearrange("p (t c) -> p t c", c=P), iota_b[:, :].unsqueeze(1).to_broadcast([P, GT, P]),
                        rec[:, bass.ds(n * GT, GT), F_T24:F_T24 + 1].to_broadcast([P, GT, P]), ALU.is_equal).then_inc(sem("one_hot_g"), 1)

                def body(n, h, q, i, first, last_pass):
                    if not (last_pass and h and q == GPH - 1):
                        hot(n + 1, (q + 1) % GPH, first and h == 0 and q < GPH - 1)
                    if q:
                        product(i, h, q - 1)
                    elif h:
                        product(i, 0, GPH - 1)
                    elif not first:
                        product(i - 1, 1, GPH - 1)
                    if q == 0:
                        if not first:
                            dve.wait_ge(sem(f"msg_scattered{h}"), 16 * HALF * i)
                        nc.vector.tensor_copy(idx_ring[:, h, :], row_of[:, bass.ds((2 * i + h) * HALF, HALF)])

                hot(0, 0, True)
                ring_steps(dve, body, peel_last=True)
                product(RINGS - 1, 1, GPH - 1)

            def source_hot():
                def body(i, first):
                    for h in range(2):
                        for q in range(GPH):
                            n, p = 2 * GPH * i + GPH * h + q, q % 2
                            if q == 0:
                                dve.wait_ge(sem(f"msg_loaded{h}"), 16 * i + 16)
                            if not (first and h == 0 and q < 2):
                                dve.wait_ge(sem("acc3"), n - 1)
                            nc.vector.tensor_tensor(ohf[:, p, :, :], iota[:, :].unsqueeze(1).to_broadcast([P, GT, P]),
                                                    ring[:, h, q * GT:q * GT + GT, D:MW].to_broadcast([P, GT, P]),
                                                    ALU.is_equal).then_inc(sem("weighted3"), 1)
                loop(dve, RINGS, body)

            projected(0)
            dve.wait_ge(sem("rec_loaded"), 16)
            dve.wait_ge(sem("msg_filled"), 16 * (T // HALF))
            dve.wait_ge(sem("rows_stored0"), 16)
            scores(0)
            weigh(0)
            norm(0)
            projected(1)
            dve.wait_ge(sem("rows_stored1"), 16)
            scores(1)
            global_max()
            weigh(1)
            norm(1)
            relations()
            for j in range(XB):
                dve.wait_ge(sem(f"rel_stored{j}"), 16 * XI)
            nc.vector.tensor_scalar(zrow, rec[:, :, F_DLOC], 0.0, float(2 * NB), ALU.is_lt, ALU.mult)
            dve.drain()
            nc.vector.tensor_tensor(key, zrow, rec[:, :, F_SHI], ALU.add)
            dve.drain()
            rank(dve, "src", key)
            weigh(2)
            norm(2)
            f = xs[:, :, :]
            y = h_sb
            dve.wait_ge(sem("w24_loaded"), 16)
            nc.vector.tensor_copy(w24f[:, :], w24[:, :])
            nc.vector.tensor_copy(y, f)
            dve.drain()
            split(y.rearrange("p b c -> p (b c)"), [xs3[:, k, :] for k in range(3)])
            split(w24f[:, :], [w24s[:, k, :] for k in range(3)])
            nc.vector.memset(small[:, 11, 3:4], 0.0).then_inc(sem("x_split"), 1)
            make_messages()
            source_hot()
            norm(3)

        @block.scalar
        def _(act):
            for h in range(H):
                act.dma_start(acol[HD * h:HD * h + HD, 0:3], att_a[h, :].rearrange("(j d) -> d j", j=3)).then_inc(sem("par_loaded"), 16)
            act.dma_start(acol[:, 3:4], att_src.rearrange("o h d -> (h d) o")).then_inc(sem("par_loaded"), 16)
            act.dma_start(acol[:, 4:5], att_tgt.rearrange("o h d -> (h d) o")).then_inc(sem("par_loaded"), 16)
            act.dma_start(w_nat[:, :], W_node).then_inc(sem("par_loaded"), 16)
            act.dma_start(we2[:, 0:KE], W_edge).then_inc(sem("par_loaded"), 16)
            act.dma_start(we2[:, KE:2 * KE], W_edge).then_inc(sem("par_loaded"), 16)
            act.dma_start(wx[:, 1, 0:D], W_proj).then_inc(sem("par_loaded"), 16)
            act.dma_start(bias_bc[:, :], proj_bias.rearrange("(o c) -> o c", o=1).to_broadcast([P, D])).then_inc(sem("par_loaded"), 16)
            act.wait_ge(sem("par_loaded"), 16 * (H + 7))
            act.wait_ge(sem("masks"), 4)
            for j in range(5):
                act.activation(aexp[:, j, :], headmask[:, :], ACT.Copy, scale=acol[:, j:j + 1])
            act.activation(wea2[:, :, :], headmask[:, :].unsqueeze(1).to_broadcast([P, 2, H]), ACT.Copy, scale=0.0)\
                .then_inc(sem("aexp"), 1)
            act.drain()
            act.wait_ge(sem("wT_made"), 1)
            act.activation(wx[:, 0, 0:D], bank(0, 0, D), ACT.Copy)
            act.activation(wpT[:, :], bank(0, D, 2 * D), ACT.Copy).then_inc(sem("wpT"), 1)
            act.wait_ge(sem("wa_made"), 1)
            act.activation(wx[:, 0, D:D + 2 * H], bank(1, 0, 2 * H), ACT.Copy)
            act.activation(wx[:, 1, D:D + 2 * H], bank(1, 32, 32 + 2 * H), ACT.Copy)
            act.activation(wea2[0:KE, 0, :], bank(1, 64, 64 + H)[0:KE, :], ACT.Copy)
            act.activation(wea2[KE:2 * KE, 1, :], bank(1, 64, 64 + H)[KE:2 * KE, :], ACT.Copy).then_inc(sem("wx_made"), 1)

            act.wait_ge(sem("msg_pat_made"), 1)
            for q in range(T // HALF):
                act.dma_start(msg_v[:, q * HALF:(q + 1) * HALF, :], msg_pat).then_inc(sem("msg_filled"), 16)

            def attr_copy(i, first):
                for h in range(2):
                    for q in range(2):
                        n = 4 * i + 2 * h + q
                        act.wait_ge(sem("attr_transposed"), n + 1)
                        if not first or h:
                            act.wait_ge(sem("eatt_quad"), n - 1)
                        act.activation(scaled[:, q, :, :].rearrange("p g c -> p (g c)"), bank(q), ACT.Copy).then_inc(sem("attrT"), 1)

            loop(act, RINGS, attr_copy)

            def turn_nodes(L):
                def body(i, first):
                    if not first:
                        hold(act, f"x_turned{L}", i)
                    act.activation(x_stage, xs[:, bass.ds(XB * i, XB), :].rearrange("p b c -> p (b c)"), ACT.Copy).then_inc(sem(f"x_staged{L}"), 1)
                    hold(act, f"x_turned{L}", i + 1)
                    if not first:
                        act.wait_ge(sem(f"proj_mm{L}" if L < 2 else "rel_mm"), i if L < 2 else XB * i)
                    act.activation(xT, PS[:, 0:XB * P], ACT.Copy).then_inc(sem(f"xT{L}"), 1)
                loop(act, XI, body)

            def stage_idx(L, i, h, field, first):
                if not first:
                    hold(act, f"gathered{L}_{h}", 16 * HALF * i)
                act.activation(idx_ring[:, h, :], rec[:, bass.ds((2 * i + h) * HALF, HALF), field], ACT.Copy).then_inc(sem(f"idx_staged{L}"), 1)

            def stage_all_idx(L, field):
                with act.Fori(1, RINGS) as i:
                    for h in range(2):
                        stage_idx(L, i, h, field, False)

            def spread_table(L):
                act.wait_ge(sem(f"tab_turned{L}"), 1)
                act.activation(tab_T[0:NB, :], bank(6)[0:NB, :], ACT.Copy).then_inc(sem(f"tab_T{L}"), 1)

            def table_half(tag, looked, i, h, first):
                if not first:
                    hold(act, looked, 2 * GPH * i + GPH * h - GPH)
                act.activation(tab_h[:, h, :, :, :], tab_t[:, bass.ds((2 * i + h) * HALF, HALF), :, :], ACT.Copy).then_inc(sem(f"tab_half_{tag}"), 1)

            def score_loop(L):
                def keep(n, p):
                    act.wait_ge(sem("parts_turned"), n + 1)
                    act.activation(apartT[0:KP, p, :], bank(2 + p, 64, 128).bitcast(bf16)[0:KP, :], ACT.Copy).then_inc(sem("partsT"), 1)
                    hold(act, "scored0", n + 1)
                    act.activation(att[:, bass.ds(n * GT, GT), :], att_g[:, p, :].rearrange("p (t h) -> p t h", h=H), ACT.Copy).then_inc(sem("att_kept"), 1)

                def step(i, first, last=False):
                    for h in range(2):
                        if h == 0 and not first:
                            stage_idx(L, i, 1, F_SRC, False)
                        elif h == 1 and not last:
                            stage_idx(L, i + 1, 0, F_SRC, False)
                        table_half(f"t{L}", f"looked{L}", i, h, first)
                        for q in range(GPH if L == 0 else 0):
                            n, p = 2 * GPH * i + GPH * h + q, q % 2
                            act.wait_ge(sem("turned"), n + 1)
                            if q == 0 and not first:
                                act.wait_ge(sem(f"hotT_saved_{h}"), 16 * i)
                            act.activation(hotT[:, h, q * GT * P:(q + 1) * GT * P], bank(p).bitcast(bf16)[:, 0:GT * P],
                                           ACT.Copy, scale=-1.0, bias=1.0).then_inc(sem("hotT_made"), 1)
                            if not (first and h == 0 and q == 0):
                                keep(n - 1, 1 - p)

                act.wait_ge(sem("tab_split"), 1 + 2 * L)
                step(0, True)
                step(1, False)
                with act.Fori(2, RINGS - 1) as i:
                    step(i, False)
                step(RINGS - 1, False, True)
                if L == 0:
                    keep(LASTG, 1)

            def weights(L):
                w = D + (2 * H if L == 0 else H)

                def part0(n, q, early):
                    act.wait_ge(sem(f"weighted{L}"), n + 1)
                    if not early:
                        act.wait_ge(sem(f"acc{L}"), n - 3)
                    act.activation(parts[q][:, 0, :, 0:w], vals[:, q, :, 0:w], ACT.Copy).then_inc(sem(f"part0_{L}"), 1)

                def part1(n, q):
                    act.wait_ge(sem(f"rest{L}"), n + 1)
                    act.activation(parts[q][:, 1, :, 0:w], vals[:, q, :, 0:w], ACT.Copy).then_inc(sem(f"part1_{L}"), 1)

                def body(n, h, q, i, first):
                    start = first and h == 0
                    if L == 0 and q == 0:
                        table_half("m", "looked_m", i, h, first)
                    if L == 0:
                        if not start:
                            act.wait_ge(sem("parts_made0"), n - 3)
                        act.wait_ge(sem("shifted"), n + 1)
                        act.activation(vals[:, q, :, D:D + H], arg_g[:, q % 2, :, :], ACT.Exp)
                        act.activation(vals[:, q, :, D + H:D + 2 * H], bank(7, 0, GT * H).rearrange("p (t h) -> p t h", h=H),
                                       ACT.Exp, scale=-1.0).then_inc(sem("weights_made0"), 1)
                    else:
                        if not start:
                            hold(act, "parts_made1", n - 3)
                        act.activation(vals[:, q, :, D:D + H], att[:, bass.ds(n * GT, GT), :], ACT.Exp, bias=small[:, 5, 2:3]).then_inc(sem("weights_made1"), 1)
                    if not (start and q < 1):
                        part0(n - 1, before(h, q)[1], first and GPH * h + q < 5)
                    if not (start and q < 2):
                        part1(n - 2, before(h, q, 2)[1])

                ring_steps(act, body)
                part0(LASTG, GPH - 1, False)
                part1(LASTG - 1, GPH - 2)
                part1(LASTG, GPH - 1)

            def std(L):
                act.wait_ge(sem("var_made"), L + 1)
                act.activation(stat[:, 6, 0:NB], stat[:, 5, 0:NB], ACT.Sqrt).then_inc(sem("std_made"), 1)

            turn_nodes(0)
            act.wait_ge(sem("rec_loaded"), 16)
            stage_idx(0, 0, 0, F_SRC, True)
            stage_idx(0, 0, 1, F_SRC, True)
            spread_table(0)
            act.wait_ge(sem("msg_filled"), 16 * (T // HALF))
            score_loop(0)
            act.wait_ge(sem("tab_split"), 2)
            weights(0)
            std(0)
            act.wait_ge(sem("normed"), 1)
            turn_nodes(1)
            for h in range(2):
                act.wait_ge(sem(f"gathered0_{h}"), 16 * HALF * RINGS)
                stage_idx(1, 0, h, F_SRC, True)
            spread_table(1)
            score_loop(1)
            act.wait_ge(sem("max_ready"), 1)
            weights(1)
            act.wait_ge(sem("parts_made1"), T // GT)
            act.dma_start(w_rel, W_rel.rearrange("r i o -> i r o")).then_inc(sem("rel_loaded"), 16)
            act.dma_start(b_rel_bc, b_rel.rearrange("r o -> (r o)").rearrange("(a c) -> a c", a=1).to_broadcast([P, R8 * D])).then_inc(sem("rel_loaded"), 16)
            std(1)
            act.wait_ge(sem("normed"), 2)
            turn_nodes(2)
            for h in range(2):
                act.wait_ge(sem(f"gathered1_{h}"), 16 * HALF * RINGS)
                stage_idx(2, 0, h, F_ROW, True)
            act.wait_ge(sem("w24_cleared"), 1)
            act.dma_start(w24[0:R24, :], rel_weight).then_inc(sem("w24_loaded"), 16)
            stage_all_idx(2, F_ROW)
            std(2)

            def rel_terms(n, p):
                act.wait_ge(sem("looked_up_g"), n + 1)
                act.activation(scaled[:, p, :, :].rearrange("p t c -> p (t c)"), bank(4 + p), ACT.Copy).then_inc(sem("rel_copied"), 1)

            def turn_message_hots(i, first):
                for p in range(2):
                    n = 2 * i + p
                    act.wait_ge(sem("transposed_g"), n + 1)
                    if not first:
                        act.wait_ge(sem("looked_up_g"), n - 1)
                    act.activation(ohT[:, p, 0, :], bank(p).bitcast(bf16)[:, 0:GT * P], ACT.Copy).then_inc(sem("ohT_g"), 1)
                    if not (first and p == 0):
                        if not first:
                            wait_free(act, "msg_made", n - 2)
                        rel_terms(n - 1, 1 - p)

            loop(act, T // GT // 2, turn_message_hots)
            rel_terms(T // GT - 1, 1)
            std(3)

        @block.tensor
        def _(pe):
            pe.wait_ge(sem("par_loaded"), 16 * (H + 7))
            pe.wait_ge(sem("masks"), 4)
            pe.transpose(bank(0, 0, D), w_nat[:, :], ident[:, :])
            pe.transpose(bank(0, D, 2 * D), wx[:, 1, 0:D], ident[:, :]).then_inc(sem("wT_made"), 1)
            pe.wait_ge(sem("aexp"), 1)
            pe.matmul(bank(1, 0, 2 * H), w_nat[:, :], aexp[:, 0:2, :].rearrange("p j h -> p (j h)"), start=True, stop=True)
            pe.wait_ge(sem("wpT"), 1)
            pe.matmul(bank(1, 32, 32 + 2 * H), wpT[:, :], aexp[:, 3:5, :].rearrange("p j h -> p (j h)"), start=True, stop=True)
            pe.matmul(bank(1, 64, 64 + H), we2[:, :], aexp[:, 2, :], start=True, stop=True).then_inc(sem("wa_made"), 1)
            pe.wait_ge(sem("dst_counted"), 1)
            pe.matmul(bank(7, 0, NB), tri[:, :], small[:, 0, 0:NB], start=True, stop=True)
            pe.matmul(bank(7, 32, 32 + NB), ones[:, :], small[:, 0, 0:NB], start=True, stop=True).then_inc(sem("dst_summed"), 1)

            pe.wait_ge(sem("wx_made"), 1)
            pe.wait_ge(sem("attr_cleared"), 1)

            def eatt(i, first):
                for h in range(2):
                    k = 2 * i + h
                    pe.wait_ge(sem(f"attr_loaded{h}"), attr_incs(i, h))
                    for q in range(2):
                        n = 2 * k + q
                        if not first or h:
                            pe.wait_ge(sem("attrT"), n - 1)
                        for j in range(4):
                            c = (4 * q + j) * 2 * KE
                            last = pe.transpose(bank(q, j * P, j * P + P), attr[:, h, c:c + 2 * KE], ident[:, :])
                        last.then_inc(sem("attr_transposed"), 1)
                    if not first:
                        pe.wait_ge(sem("rec_staged"), k - 1)
                    for q in range(2):
                        pe.wait_ge(sem("attrT"), 2 * k + q + 1)
                        for j in range(4):
                            c = (4 * q + j) * 2 * H
                            last = pe.matmul(bank(2 + h, c, c + 2 * H), scaled[:, q, j, :],
                                             wea2[:, :, :].rearrange("p a h -> p (a h)"), start=True, stop=True)
                        last.then_inc(sem("eatt_quad"), 1)

            def attr_incs(i, h):
                if not isinstance(i, int):
                    return 32 * i + 32
                return sum(32 if EREST > (2 * j + h) * HALF else 16 for j in range(i + 1))

            whole = EREST // (2 * HALF)
            eatt(0, True)
            with pe.Fori(1, whole) as i:
                eatt(i, False)
            for i in range(whole, RINGS):
                eatt(i, False)

            def turn_nodes(L, i, first):
                pe.wait_ge(sem(f"x_staged{L}"), i + 1)
                if not first:
                    pe.wait_ge(sem(f"xT{L}"), i)
                for j in range(XB):
                    last = pe.transpose(PS[:, j * P:j * P + P], x_stage[:, j * P:j * P + P], ident[:, :])
                last.then_inc(sem(f"x_turned{L}"), 1)
                pe.wait_ge(sem(f"xT{L}"), i + 1)

            def project(L):
                def body(i, first):
                    turn_nodes(L, i, first)
                    if not first:
                        pe.wait_ge(sem(f"projected{L}"), i)
                    for j in range(XB):
                        c = (j % 3) * PC
                        last = pe.matmul(bank(2 + j // 3, c, c + PC), xT[:, j * P:j * P + P], wx[:, L, :], start=True, stop=True)
                    last.then_inc(sem(f"proj_mm{L}"), 1)
                loop(pe, XI, body)

            def blocks_of(n, row):
                _, blocks = nc.values_load_multi_w_load_instructions(
                    row[0:1, bass.ds(n * GT, GT)], engines=[pe.engine], min_val=0, max_val=NB - 1,
                    skip_runtime_bounds_check_because="the ranking writes block numbers from 0 to NB - 1 only")
                return blocks

            def spread_table(L):
                pe.wait_ge(sem(f"projected{L}"), XI)
                for h in range(H):
                    last = pe.transpose(bank(6, h * P, h * P + P)[0:NB, :], tab_f[:, h, :], ident[:, :])
                last.then_inc(sem(f"tab_turned{L}"), 1)
                pe.wait_ge(sem(f"tab_T{L}"), 1)
                pe.wait_ge(sem(f"blk_hot{L}"), 1)
                for h in range(H):
                    for c in range(2):
                        pe.matmul(bank(2 * h + c, 0, MID), tab_T[0:NB, h * P:h * P + P], blk_hot[0:NB, c * MID:c * MID + MID],
                                  start=True, stop=True).then_inc(sem(f"tab_mm{L}"), 1)
                pe.wait_ge(sem("tab_split"), 1 + 2 * L)

            def look_up(out, h, q):
                for t in range(GT):
                    c = (q * GT + t) * P
                    for k in range(3):
                        last = pe.matmul(out[:, t * H:t * H + H], hotT[:, h, c:c + P], tab_h[:, h, q * GT + t, k, :],
                                         start=(k == 0), stop=(k == 2))
                return last

            def scores0():
                def look(n, h, q, i, early):
                    p = q % 2
                    pe.wait_ge(sem("hotT_made"), n + 1)
                    if q == 0:
                        pe.wait_ge(sem("tab_half_t0"), 2 * i + h + 1)
                    if not early:
                        pe.wait_ge(sem("scored0"), n - 1)
                    look_up(bank(2 + p, 0, GT * H), h, q).then_inc(sem("looked0"), 1)

                def spread(n, q, early):
                    p = q % 2
                    pe.wait_ge(sem("partsT"), n + 1)
                    for t in range(GT):
                        if t % 2 == 0 and not early:
                            pe.wait_ge(sem("maxed"), 2 * n - 1 + t // 2)
                        pe.matmul(bank(4 + t), hot4(q)[:, t * P:t * P + P], far_id[:, :, :].rearrange("p h c -> p (h c)"),
                                  start=True, stop=False, skip_group_check=True)
                        for h in range(H):
                            last = pe.matmul(bank(4 + t, h * P, h * P + P), pick[0:KP, t * H + h, :], apartT[0:KP, p, :],
                                             start=False, stop=True, skip_group_check=True)
                        if t % 2:
                            last.then_inc(sem("spread"), 1)

                def turn_parts(n, q):
                    pe.wait_ge(sem("scored0"), n + 1)
                    pe.transpose(bank(2 + q % 2, 64, 128).bitcast(bf16), apart[:, q % 2, :], ident_b[:, :]).then_inc(sem("parts_turned"), 1)

                def body(n, h, q, i, first):
                    p, start = q % 2, first and h == 0
                    pe.wait_ge(sem("hot_made"), n + 1)
                    if not (start and q < 2):
                        pe.wait_ge(sem("hotT_made"), n - 1)
                    for t in range(GT):
                        last = pe.transpose(bank(p).bitcast(bf16)[:, t * P:t * P + P], hot4(q)[:, t * P:t * P + P], ident_b[:, :])
                    last.then_inc(sem("turned"), 1)
                    h1, q1 = before(h, q)
                    h2, q2 = before(h1, q1)
                    if not (start and q == 0):
                        look(n - 1, h1, q1, i, start and q < 3)
                    if not (start and q < 2):
                        spread(n - 2, q2, start and q < 3)
                    if not (start and q == 0):
                        turn_parts(n - 1, q1)

                ring_steps(pe, body)
                look(LASTG, 1, GPH - 1, RINGS - 1, False)
                spread(LASTG - 1, GPH - 2, False)
                turn_parts(LASTG, GPH - 1)
                spread(LASTG, GPH - 1, False)

            def scores1():
                def body(n, h, q, i, first):
                    if q == 0:
                        pe.wait_ge(sem(f"hotT_loaded1_{h}"), 16 * i + 16)
                        pe.wait_ge(sem("tab_half_t1"), 2 * i + h + 1)
                    if not (first and h == 0 and q < 2):
                        pe.wait_ge(sem("scored1"), n - 1)
                    look_up(bank(2 + q % 2, 0, GT * H), h, q).then_inc(sem("looked1"), 1)
                ring_steps(pe, body)

            def clear_sums():
                for k in range(ACC_BANKS):
                    pe.matmul(bank(k), zeros[:, 0:P], zeros[:, :], start=True, stop=True)

            def weighted_sums(L):
                ns = 2 * H if L == 0 else H

                def add(n, q):
                    pe.wait_ge(sem(f"parts_made{L}"), n + 1)
                    blocks = blocks_of(n, blk_dst)
                    for t in range(GT):
                        hot = hot4(q)[:, t * P:t * P + P]
                        for k in range(3):
                            pe.matmul(PS[:, bass.ds(blocks[t] * D, D)], hot, parts[q][:, k, t, 0:D],
                                      start=False, stop=True, skip_group_check=True)
                        for k in range(3):
                            m = ns + 1 if L == 0 and k == 0 else ns
                            last = pe.matmul(PS[:, bass.ds(blocks[t] * NS + SUM0, m)], hot, parts[q][:, k, t, D:D + m],
                                             start=False, stop=True, skip_group_check=True)
                    last.then_inc(sem(f"acc{L}"), 1)

                def body(n, h, q, i, first):
                    start = first and h == 0
                    if L == 0:
                        if q == 0:
                            pe.wait_ge(sem(f"hotT_loaded0_{h}"), 16 * i + 16)
                            pe.wait_ge(sem("tab_half_m"), 2 * i + h + 1)
                        if not (start and q == 0):
                            pe.wait_ge(sem("weights_made0"), n)
                        look_up(bank(7, 0, GT * H), h, q).then_inc(sem("looked_m"), 1)
                    if not start:
                        add(n - GPH, q)

                ring_steps(pe, body)
                for q in range(GPH):
                    add(T // GT - GPH + q, q)

            def accumulate(L, row):
                def body(n, h, q, i, first):
                    if q == 0 and L == 2:
                        pe.wait_ge(sem(f"gathered{L}_{h}"), 16 * HALF * i + 16 * HALF)
                    pe.wait_ge(sem(f"weighted{L}"), n + 1)
                    blocks = blocks_of(n, row)
                    for t in range(GT):
                        last = pe.matmul(PS[:, bass.ds(blocks[t] * D, D)], ohf[:, q % 2, t, :], ring[:, h, q * GT + t, 0:D],
                                         start=False, stop=True, skip_group_check=True)
                    last.then_inc(sem(f"acc{L}"), 1)

                ring_steps(pe, body)

            pe.wait_ge(sem("rec_staged"), 2 * RINGS)
            pe.wait_ge(sem("attrT"), 4 * RINGS)
            pe.wait_ge(sem("x_loaded"), 32)
            project(0)
            spread_table(0)
            scores0()
            pe.wait_ge(sem("maxed"), 2 * (T // GT))
            pe.wait_ge(sem("blk_loaded"), 16)
            clear_sums()
            weighted_sums(0)
            pe.wait_ge(sem("normed"), 1)
            project(1)
            spread_table(1)
            scores1()
            pe.wait_ge(sem("lane_max"), 1)
            pe.matmul(bank(7, 0, P)[0:1, :], small[:, 5, 0:1], ident[:, :], start=True, stop=True).then_inc(sem("lane_max_turned"), 1)
            pe.wait_ge(sem("one_max"), 1)
            pe.matmul(bank(7, P, P + 1), ones[0:1, :], small[0:1, 5, 1:2], start=True, stop=True).then_inc(sem("max_spread"), 1)
            clear_sums()
            weighted_sums(1)
            pe.wait_ge(sem("normed"), 2)
            pe.wait_ge(sem("rel_loaded"), 32)

            def relate(i, first):
                turn_nodes(2, i, first)
                for j in range(XB):
                    n = XB * i + j
                    if not first or j > 2:
                        pe.wait_ge(sem("rel_made"), n - 1)
                    for k in range(2):
                        last = pe.matmul(bank(2 + 2 * (j % 3) + k), xT[:, j * P:j * P + P],
                                         w_rel.rearrange("p r c -> p (r c)")[:, k * BK:(k + 1) * BK], start=True, stop=True)
                    last.then_inc(sem("rel_mm"), 1)

            loop(pe, XI, relate)
            pe.wait_ge(sem("rel_made"), NB)
            pe.wait_ge(sem("src_counted"), 1)
            pe.matmul(bank(7, 0, NB), tri[:, :], small[:, 0, 0:NB], start=True, stop=True)
            pe.matmul(bank(7, 32, 32 + NB), ones[:, :], small[:, 0, 0:NB], start=True, stop=True).then_inc(sem("src_summed"), 1)
            pe.wait_ge(sem("xT2"), XI)
            clear_sums()
            accumulate(2, blk_dst)
            pe.wait_ge(sem("x_split"), 1)

            def message_terms(n, h, q, i, early):
                p = q % 2
                pe.wait_ge(sem("ohT_g"), n + 1)
                if q == 0:
                    pe.wait_ge(sem(f"hotT_loaded3_{h}"), 16 * i + 16)
                if not early:
                    pe.wait_ge(sem("rel_copied"), n - 1)
                    pe.wait_ge(sem("msg_made"), n - 1)
                blocks = blocks_of(n, blk_dst)
                for t in range(GT):
                    c = (q * GT + t) * P
                    for k in range(3):
                        pe.matmul(bank(2 + p, t * P, t * P + P), hotT[:, h, c:c + P],
                                  xs3[:, k, bass.ds(blocks[t] * D, D)], start=(k == 0), stop=(k == 2))
                    for k in range(3):
                        last = pe.matmul(bank(4 + p, t * P, t * P + P), ohT[:, p, 0, t * P:t * P + P], w24s[:, k, :],
                                         start=(k == 0), stop=(k == 2))
                last.then_inc(sem("looked_up_g"), 1)

            def message_body(n, h, q, i, first):
                p, start = q % 2, first and h == 0
                pe.wait_ge(sem("one_hot_g"), n + 1)
                if not (start and q < 2):
                    pe.wait_ge(sem("ohT_g"), n - 1)
                for t in range(GT):
                    last = pe.transpose(bank(p).bitcast(bf16)[:, t * P:t * P + P], hot4(q)[:, t * P:t * P + P], ident_b[:, :])
                last.then_inc(sem("transposed_g"), 1)
                if not (start and q == 0):
                    message_terms(n - 1, *before(h, q), i, start and q < 3)

            ring_steps(pe, message_body)
            message_terms(LASTG, 1, GPH - 1, RINGS - 1, False)
            pe.wait_ge(sem("msg_made"), T // GT)
            pe.wait_ge(sem("blk_loaded"), 32)
            clear_sums()
            accumulate(3, blk_src)


KIND = "Internal"

_INS = ['x', 'src', 'dst', 'edge_attr_64', 'edge_type_24', 'edge_type_8', 'edge_weight1', 'L0_gnn_W_node',
        'L0_gnn_W_edge', 'L0_gnn_a', 'L1_gnn_W_proj', 'L1_gnn_a_src', 'L1_gnn_a_tgt', 'L1_gnn_bias', 'L2_gnn_W',
        'L2_gnn_b', 'L3_gnn_weight']


def kernel(**inputs):
    import numpy as _np
    import concourse.bacc as _bacc
    from concourse import mybir as _mybir
    from concourse.bass_utils import run_bass_kernel_spmd as _run

    nc = _bacc.Bacc("TRN2", target_bir_lowering=False, num_devices=1)
    arrays, args = {}, []
    for name in _INS:
        a = _np.ascontiguousarray(inputs[name])
        arrays[f"in_{name}_dram"] = a
        args.append(nc.dram_tensor(f"in_{name}_dram", a.shape, _mybir.dt.from_np(a.dtype), kind="ExternalInput").ap())
    args.append(nc.dram_tensor("out_dram", (3125, 128), _mybir.dt.float32, kind="ExternalOutput").ap())
    gnn_resnorm_kernel(nc, *args)
    r = _run(nc, [arrays], core_ids=[0])
    return r.results[0]["out_dram"]
```

```python
import concourse.bass as bass
from concourse import mybir
from contextlib import ExitStack


def gnn_resnorm_kernel(
    nc: bass.Bass,
    x: bass.AP,
    src: bass.AP,
    dst: bass.AP,
    edge_attr: bass.AP,
    edge_type_24: bass.AP,
    edge_type_8: bass.AP,
    edge_weight: bass.AP,
    W_node: bass.AP,
    W_edge: bass.AP,
    att_a: bass.AP,
    W_proj: bass.AP,
    att_src: bass.AP,
    att_tgt: bass.AP,
    proj_bias: bass.AP,
    W_rel: bass.AP,
    b_rel: bass.AP,
    rel_weight: bass.AP,
    out: bass.AP,
):
    fp32 = mybir.dt.float32
    bf16 = mybir.dt.bfloat16
    i32 = mybir.dt.int32
    ALU = mybir.AluOpType
    ACT = mybir.ActivationFunctionType
    AX = mybir.AxisListType

    P = 128
    N, D = x.shape
    E = src.shape[0]
    KE = edge_attr.shape[1]
    H = att_a.shape[0]
    HD = D // H
    R8 = W_rel.shape[0]
    R24 = rel_weight.shape[0]
    EPS = 1e-5
    NB = -(-N // P)
    NPAD = NB * P
    NLAST = N - (NB - 1) * P
    HALF = 16
    GT = 4
    GPH = HALF // GT
    T = -(-(-(-(E + NB * (P - 1)) // P)) // (2 * HALF)) * (2 * HALF)
    RINGS = T // (2 * HALF)
    TPAD = -(-T // P) * P
    TG = TPAD // P
    EFULL = E // T
    EREST = E - EFULL * T
    FW = 16
    F_SRC, F_ROW, F_SLO, F_SHI, F_DLOC, F_T24, F_NORM, F_EATT = 0, 1, 2, 3, 4, 5, 6, 8
    MW = D + 1
    RW = D + H
    NS = 2 * H + 1
    VW = D + NS
    HG = HALF * P
    POS_PAD = float(P * 8192 + P - 1)
    ROWS = P * T
    XB = 5
    XI = NB // XB
    assert NB % XB == 0 and (P - 1) * T + 8192 >= ROWS
    HUGE = 1.0e30
    BIG = 2.0 ** 100
    KP = 3 * GT * H

    ctx = ExitStack()
    with ctx:
        ctx.enter_context(nc.allow_non_contiguous_dma(reason="attention vectors laid on partitions"))

        def sb(name, shape, dt=fp32):
            return ctx.enter_context(nc.sbuf_tensor(name, shape, dt))

        sems = {}

        def sem(name):
            if name not in sems:
                sems[name] = ctx.enter_context(nc.semaphore(name))
            return sems[name]

        records = nc.dram_tensor("records", (ROWS, FW), fp32, kind=KIND).ap()
        node_rows = nc.dram_tensor("node_rows", (NPAD, RW), fp32, kind=KIND).ap()
        rel_rows = nc.dram_tensor("rel_rows", (R8 * NPAD, D), fp32, kind=KIND).ap()
        messages = nc.dram_tensor("messages", (ROWS, MW), fp32, kind=KIND).ap()
        edge_rows = nc.dram_tensor("edge_rows", (P, T, RW), fp32, kind=KIND).ap()
        hotT_rows = nc.dram_tensor("hotT_rows", (P, T * P), bf16, kind=KIND).ap()
        blk_rows = nc.dram_tensor("blk_rows", (2, TPAD), i32, kind=KIND).ap()

        rec = sb("rec", [P, T, FW])
        xs = sb("xs", [P, NB, D])
        hbuf = sb("hbuf", [P, T * H])
        h_sb = hbuf[:, 0:NB * D].rearrange("p (b c) -> p b c", c=D)
        rows_sb = hbuf[:, 0:NB * RW].rearrange("p (b c) -> p b c", c=RW)
        att2 = hbuf[:, :].rearrange("p (t h) -> p t h", h=H)
        att = sb("att", [P, T, H])[:, :, :]
        arg_g = sb("arg_g", [P, 2, GT, H])
        pre_g = sb("pre_g", [P, 2, GT, H])
        att_g = sb("att_g", [P, 2, GT * H])
        apart = sb("apart", [P, 2, P], bf16)
        apartT = sb("apartT", [P, 2, P], bf16)
        tab_h = sb("tab_h", [P, 2, HALF, 3, H], bf16)
        far_id = sb("far_id", [P, H, P], bf16)
        ring = sb("ring", [P, 2, HALF, RW])
        idx_ring = sb("idx_ring", [P, 2, HALF], i32)
        row_of = sb("row_of", [P, T], i32)
        blk_dst = sb("blk_dst", [1, TPAD], i32)
        blk_src = sb("blk_src", [1, TPAD], i32)
        oh = sb("oh", [P, 2, 2, GT * P], bf16)
        ohT = sb("ohT", [P, 2, 2, GT * P], bf16)
        ohf = sb("ohf", [P, 2, GT, P])
        scaled = sb("scaled", [P, 2, GT, P])
        iota = sb("iota", [P, P])
        iota_b = sb("iota_b", [P, P], bf16)
        ident = sb("ident", [P, P])
        ident_b = sb("ident_b", [P, P], bf16)
        tri = sb("tri", [P, P])
        ones = sb("ones", [P, P])
        zeros = sb("zeros", [P, 512], bf16)
        tval = sb("tval", [P, TG])
        headmask = sb("headmask", [P, H])
        acol = sb("acol", [P, 5])
        aexp = sb("aexp", [P, 5, H])
        w_nat = sb("w_nat", [P, D])
        we2 = sb("we2", [P, 2 * KE])
        wea2 = sb("wea2", [P, 2, H])
        wpT = sb("wpT", [P, D])
        wx = sb("wx", [P, 2, D + 2 * H])
        w24 = sb("w24", [P, D])
        w24s = sb("w24s", [P, 3, D], bf16)
        bias_bc = sb("bias_bc", [P, D])
        stat = sb("stat", [P, 8, NB * NS])
        tab_f = sb("tab_f", [P, H, NB])
        small = sb("small", [P, 12, 32])
        small_i = sb("small_i", [P, 2, 32], i32)
        blk_w = sb("blk_w", [P, TG, NB - 1])
        blk_i = sb("blk_i", [P, TG], i32)
        TABW = T * 3 * H // 2
        AW = TABW + HG + 3 * T + T * H + 8
        arena = sb("arena", [P, AW])
        raw = arena[:, 0:5 * T].rearrange("p (f t) -> p f t", t=T)
        o = 5 * T
        key = arena[:, o:o + T]
        posf = arena[:, o + T:o + 2 * T]
        msk = arena[:, o + 2 * T:o + 4 * T].rearrange("p (a t) -> p a t", t=T)
        scn = arena[:, o + 4 * T:o + 6 * T].rearrange("p (a t) -> p a t", t=T)
        zrow = arena[:, o + 6 * T:o + 7 * T]
        o += 7 * T
        attr = arena[:, o:o + 2 * HALF * KE].rearrange("p (a w) -> p a w", a=2)
        assert o + 2 * HALF * KE <= AW
        tab_t = arena[:, 0:TABW].bitcast(bf16).rearrange("p (t k h) -> p t k h", k=3, h=H)
        hotT = arena[:, TABW:TABW + HG].bitcast(bf16).rearrange("p (a w) -> p a w", a=2)
        w0 = TABW + HG
        blk_all = arena[:, w0:w0 + T].bitcast(i32)
        same = arena[:, w0 + T:w0 + 2 * T + 1]
        blk_hot = arena[:, w0 + T:w0 + 2 * T]
        back = arena[:, w0 + 2 * T + 8:w0 + 3 * T + 8]
        tab_w = arena[:, w0 + 3 * T + 8:w0 + 3 * T + 8 + T * H].rearrange("p (t h) -> p t h", h=H)

        PS = ctx.enter_context(nc.psum_tensor("PS", [P, 4096], fp32))
        BK = 512

        def bank(i, a=0, b=BK):
            return PS[:, i * BK + a:i * BK + b]

        blk_f = small[:, 4, 0:TG]

        def rec_ring(h):
            return ring[:, h, :, :].rearrange("p t w -> p (t w)")[:, 0:HALF * FW].rearrange("p (t f) -> p t f", f=FW)

        block = ctx.enter_context(nc.Block())

        def loop(eng, n, body):
            body(0, True)
            body(1, False)
            with eng.Fori(2, n) as i:
                body(i, False)

        def ring_steps(eng, body, peel_last=False):
            def step(i, first, *last):
                for h in range(2):
                    for q in range(GPH):
                        body(2 * GPH * i + GPH * h + q, h, q, i, first, *last)
            if peel_last:
                step(0, True, False)
                step(1, False, False)
                with eng.Fori(2, RINGS - 1) as i:
                    step(i, False, False)
                step(RINGS - 1, False, True)
            else:
                loop(eng, RINGS, step)

        def hot4(q):
            return oh[:, q // 2, q % 2, :]

        SUM_AT = 2 + -(-NB // 2)
        POS_AT = SUM_AT + 1
        ROWS_AT = POS_AT + -(-NB // 3)
        assert ROWS_AT < RINGS and 3 * (ROWS_AT - POS_AT) <= NB + 4

        def before(h, q, k=1):
            j = (GPH * h + q - k) % (2 * GPH)
            return j // GPH, j % GPH

        LASTG = T // GT - 1

        PC = D + 2 * H
        SUM0 = NB * D
        ACC_BANKS = -(-(SUM0 + NB * NS) // BK)
        o = w0 + 3 * T + 8
        att_h = att[:, 0:2 * HALF, :].rearrange("p (a t) h -> p a t h", a=2)
        CUT = 2 * BK
        vals = arena[:, o:o + GPH * GT * VW].rearrange("p (a t c) -> p a t c", a=GPH, c=VW)
        SW = 3 * GT * VW // 2
        assert SW <= 2 * T and SW <= 2 * GT * P and GPH * GT * VW + SW <= T * H
        parts = [a.bitcast(bf16).rearrange("p (k t c) -> p k t c", k=3, c=VW) for a in (
            arena[:, o + GPH * GT * VW:o + GPH * GT * VW + SW], arena[:, w0 + T:w0 + T + SW],
            ohf[:, :, :, :].rearrange("p a t c -> p (a t c)")[:, 0:SW],
            scaled[:, :, :, :].rearrange("p a t c -> p (a t c)")[:, 0:SW])]
        tab_T = ohf[:, :, :, :].rearrange("p a t c -> p (a t c)")[:, 0:H * P]
        pick = ohT[:, :, :, :].rearrange("p a k c -> p (a k c)").rearrange("p (j c) -> p j c", c=P)
        MID = T // 2
        assert MID <= BK and KP <= P
        w24f = sb("w24f", [P, D])
        x_stage = ohf[:, :, :, :].rearrange("p a t c -> p (a t c)")[:, 0:XB * P]
        xT = scaled[:, :, :, :].rearrange("p a t c -> p (a t c)")[:, 0:XB * P]
        rel_stage = arena[:, 0:XB * R8 * D].rearrange("p (j w) -> p j w", j=XB)
        w_rel = arena[:, o:o + R8 * D].rearrange("p (r c) -> p r c", r=R8)
        b_rel_bc = arena[:, o + R8 * D:o + 2 * R8 * D]
        assert o + 2 * R8 * D <= AW
        xs3 = arena[:, 0:3 * NB * D // 2].bitcast(bf16).rearrange("p (k c) -> p k c", k=3)
        msg_v = messages.rearrange("(p t) w -> p t w", t=T)
        msg_pat = att[:, :, :].rearrange("p t s -> p (t s)")[:, 0:HALF * MW].rearrange("p (t w) -> p t w", w=MW)

        def hold(eng, name, value):
            eng.wait_ge(sem(name), value)
            eng.sem_inc(sem(f"held_{eng_name(eng)}"), 1)

        def eng_name(eng):
            return str(eng.engine).split(".")[-1]

        IN_F = ("src", "dst", "t8", "t24", "w1")

        @block.sync
        def _(sp):
            sp.wait_ge(sem("raw_cleared"), 1)
            for f, a in enumerate((src, dst, edge_type_8, edge_type_24, edge_weight.rearrange("e o -> (e o)"))):
                to = raw[:, f, :] if f == 4 else raw[:, f, :].bitcast(i32)
                sp.dma_start(to[0:EFULL, :], a[0:EFULL * T].rearrange("(p t) -> p t", t=T)).then_inc(sem("raw_loaded"), 16)
                sp.dma_start(to[EFULL:EFULL + 1, 0:EREST], a[EFULL * T:E].rearrange("(o t) -> o t", o=1)).then_inc(sem("raw_loaded"), 16)
            sp.wait_ge(sem("xs_cleared"), 1)
            sp.dma_start(xs[:, 0:NB - 1, :], x[0:(NB - 1) * P, :].rearrange("(b p) c -> p b c", p=P)).then_inc(sem("x_loaded"), 16)
            sp.dma_start(xs[0:NLAST, NB - 1, :], x[(NB - 1) * P:N, :]).then_inc(sem("x_loaded"), 16)
            sp.wait_ge(sem("blk_made"), 1)
            sp.dma_start(blk_rows[0, :].rearrange("(g p) -> p g", p=P), blk_i[:, :]).then_inc(sem("blk_stored"), 16)
            sp.wait_ge(sem("blk_stored"), 16)
            sp.dma_start(blk_dst[:, :], blk_rows[0:1, :]).then_inc(sem("blk_loaded"), 16)

            ea_full = edge_attr[0:EFULL * T, :].rearrange("(p t) k -> p (t k)", t=T)
            ea_rest = edge_attr[EFULL * T:E, :].rearrange("(o t) k -> o (t k)", o=1)
            CW = HALF * KE

            def attr_load(i, first):
                for h in range(2):
                    if not first:
                        sp.wait_ge(sem("attr_transposed"), 4 * i + 2 * h - 2)
                    c = (2 * i + h) * CW
                    sp.dma_start(attr[0:EFULL, h, :], ea_full[:, bass.ds(c, CW)]).then_inc(sem(f"attr_loaded{h}"), 16)
                    n = CW if not isinstance(i, int) or first else min(max(EREST * KE - c, 0), CW)
                    if n:
                        sp.dma_start(attr[EFULL:EFULL + 1, h, 0:n], ea_rest[:, bass.ds(c, n)]).then_inc(sem(f"attr_loaded{h}"), 16)

            whole = EREST // (2 * HALF)
            attr_load(0, True)
            with sp.Fori(1, whole) as i:
                attr_load(i, False)
            for i in range(whole, RINGS):
                attr_load(i, False)
            for h in range(2):
                sp.wait_ge(sem(f"rec_scattered{h}"), 16 * HALF * RINGS)
            sp.dma_start(rec[:, :, :], records.rearrange("(p t) f -> p t f", t=T)).then_inc(sem("rec_loaded"), 16)
            sp.wait_ge(sem("blk_loaded"), 16)
            sp.dma_start(blk_all, blk_rows[0:1, 0:T].to_broadcast([P, T])).then_inc(sem("blk_spread"), 16)

            def load_hots(L, used):
                def body(i, first):
                    for h in range(2):
                        if not first:
                            sp.wait_ge(sem(used), 2 * GPH * i + GPH * h - GPH)
                        sp.dma_start(hotT[:, h, :], hotT_rows[:, bass.ds((2 * i + h) * HG, HG)]).then_inc(sem(f"hotT_loaded{L}_{h}"), 16)
                loop(sp, RINGS, body)

            for L in range(2):
                sp.wait_ge(sem(f"projected{L}"), XI)
                sp.dma_start(node_rows.rearrange("(b p) c -> p b c", p=P), rows_sb).then_inc(sem(f"rows_stored{L}"), 16)

                if L == 1:
                    load_hots(1, "looked1")
                    continue

                def save(i, first):
                    for h in range(2):
                        sp.wait_ge(sem(f"gathered0_{h}"), 16 * HALF * i + 16 * HALF)
                        sp.dma_start(edge_rows[:, bass.ds((2 * i + h) * HALF, HALF), :], ring[:, h, :, :]).then_inc(sem(f"saved0_{h}"), 16)
                        sp.wait_ge(sem("hotT_made"), 2 * GPH * i + GPH * h + GPH)
                        sp.dma_start(hotT_rows[:, bass.ds((2 * i + h) * HG, HG)], hotT[:, h, :]).then_inc(sem(f"hotT_saved_{h}"), 16)

                loop(sp, RINGS, save)
                for h in range(2):
                    sp.wait_ge(sem(f"saved0_{h}"), 16 * RINGS)
                    sp.wait_ge(sem(f"hotT_saved_{h}"), 16 * RINGS)
                sp.wait_ge(sem("scored0"), T // GT)

                def reload(i, first):
                    for h in range(2):
                        if not first:
                            sp.wait_ge(sem("looked_m"), 2 * GPH * i + GPH * h - GPH)
                        sp.dma_start(hotT[:, h, :], hotT_rows[:, bass.ds((2 * i + h) * HG, HG)]).then_inc(sem(f"hotT_loaded0_{h}"), 16)
                        if not first:
                            sp.wait_ge(sem("weighted0"), 2 * GPH * i + GPH * h - GPH)
                        sp.dma_start(ring[:, h, :, :], edge_rows[:, bass.ds((2 * i + h) * HALF, HALF), :]).then_inc(sem(f"rows_loaded0_{h}"), 16)

                loop(sp, RINGS, reload)
            rel_v = rel_rows.rearrange("(r b p) c -> p b r c", b=NB, p=P)

            def rel_store(i, first):
                for j in range(XB):
                    sp.wait_ge(sem("rel_made"), XB * i + j + 1)
                    sp.dma_start(rel_v[:, bass.ds(XB * i + j, 1), :, :], rel_stage[:, j, :].rearrange("p (o r c) -> p o r c", o=1, c=D))\
                        .then_inc(sem(f"rel_stored{j}"), 16)

            loop(sp, XI, rel_store)
            sp.wait_ge(sem("blk_made"), 2)
            sp.dma_start(blk_rows[1, :].rearrange("(g p) -> p g", p=P), blk_i[:, :]).then_inc(sem("blk_stored"), 16)
            sp.wait_ge(sem("blk_stored"), 32)
            sp.dma_start(blk_src[:, :], blk_rows[1:2, :]).then_inc(sem("blk_loaded"), 16)
            sp.wait_ge(sem("normed"), 3)
            load_hots(3, "looked_up_g")
            for h in range(2):
                sp.wait_ge(sem(f"msg_scattered{h}"), 16 * HALF * RINGS)

            def load_messages(i, first):
                for h in range(2):
                    if not first:
                        sp.wait_ge(sem("acc3"), 2 * GPH * i + GPH * h - GPH)
                    sp.dma_start(ring[:, h, :, 0:MW], msg_v[:, bass.ds((2 * i + h) * HALF, HALF), :]).then_inc(sem(f"msg_loaded{h}"), 16)

            loop(sp, RINGS, load_messages)
            sp.wait_ge(sem("normed"), 4)
            sp.dma_start(out[0:(NB - 1) * P, :].rearrange("(b p) c -> p b c", p=P), xs[:, 0:NB - 1, :]).then_inc(sem("out_stored"), 16)
            sp.dma_start(out[(NB - 1) * P:N, :], xs[0:NLAST, NB - 1, :]).then_inc(sem("out_stored"), 16)
            sp.wait_ge(sem("out_stored"), 32)

        @block.gpsimd
        def _(pool):
            pool.memset(arena[:, 0:5 * T].bitcast(i32), 0).then_inc(sem("raw_cleared0"), 1)
            pool.memset(xs[:, :, :], 0.0).then_inc(sem("xs_cleared"), 1)
            pool.memset(attr[:, :, :], 0.0).then_inc(sem("attr_cleared"), 1)
            pool.wait_ge(sem("raw_cleared0"), 1)
            pool.memset(raw[:, 1, :].bitcast(i32), NPAD + P).then_inc(sem("raw_cleared"), 1)
            pool.memset(ring[:, :, :, :], 0.0).then_inc(sem("ring_cleared"), 1)
            pool.memset(ones[:, :], 1.0).then_inc(sem("ones"), 1)
            pool.wait_ge(sem("ring_cleared"), 1)
            pat = ring[:, 0, :, 0:FW]
            pool.memset(ring[:, 0, :, F_DLOC:F_DLOC + 1], -1.0).then_inc(sem("pat_made"), 1)
            pool.iota(iota[:, :], [[1, P]], base=0, channel_multiplier=0, allow_small_or_imprecise_dtypes=True).then_inc(sem("iota"), 1)
            pool.iota(tval[:, :], [[P, TG]], base=0, channel_multiplier=1, allow_small_or_imprecise_dtypes=True).then_inc(sem("iota"), 1)
            pool.wait_ge(sem("ones"), 1)
            pool.affine_select(out=tri[:, :], in_=ones[:, :], compare_op=ALU.is_gt, fill=0.0, base=0,
                               pattern=[[1, P]], channel_multiplier=-1).then_inc(sem("masks"), 1)
            pool.affine_select(out=ident[:, :], in_=ones[:, :], compare_op=ALU.is_equal, fill=0.0, base=0,
                               pattern=[[1, P]], channel_multiplier=-1).then_inc(sem("masks"), 1)
            pool.affine_select(out=headmask[:, :], in_=ones[:, 0:H], compare_op=ALU.is_ge, fill=0.0, base=0,
                               pattern=[[-HD, H]], channel_multiplier=1).then_inc(sem("masks"), 1)
            pool.wait_ge(sem("masks"), 3)
            pool.affine_select(out=headmask[:, :], in_=headmask[:, :], compare_op=ALU.is_ge, fill=0.0, base=HD - 1,
                               pattern=[[HD, H]], channel_multiplier=-1).then_inc(sem("masks"), 1)
            pool.wait_ge(sem("pat_made"), 1)
            steps = T // HALF
            for q in range(steps):
                pool.dma_start(records.rearrange("(p s t) f -> p s t f", p=P, s=steps)[:, q, :, :], pat).then_inc(sem("rec_filled"), 16)
            pool.wait_ge(sem("rec_filled"), 16 * steps)

            last_row = pool.to_reg(ROWS - 1)

            def scatter_records(i, first):
                for h in range(2):
                    hold(pool, "rec_staged", 2 * i + h + 1)
                    for t in range(HALF):
                        pool.indirect_dma_start(
                            out=records[:, :], out_offset=bass.IndirectOffsetOnAxis(ap=idx_ring[:, h, t:t + 1], axis=0),
                            in_=rec_ring(h)[:, t, :], in_offset=None,
                            bounds_check=last_row, oob_is_err=False).then_inc(sem(f"rec_scattered{h}"), 16)

            loop(pool, RINGS, scatter_records)
            def gather(L, table, w, freed):
                def body(i, first):
                    for h in range(2):
                        hold(pool, f"idx_staged{L}", 2 * i + h + 1)
                        if not first:
                            hold(pool, freed, 2 * GPH * i + GPH * h - GPH)
                            if L == 0:
                                hold(pool, f"saved0_{h}", 16 * i)
                        for t in range(HALF):
                            pool.indirect_dma_start(
                                out=ring[:, h, t, 0:w], out_offset=None, in_=table,
                                in_offset=bass.IndirectOffsetOnAxis(ap=idx_ring[:, h, t:t + 1], axis=0))\
                                .then_inc(sem(f"gathered{L}_{h}"), 16)
                loop(pool, RINGS, body)

            for L in range(2):
                pool.wait_ge(sem(f"rows_stored{L}"), 16)
                gather(L, node_rows[:, :], RW, "scored0" if L == 0 else "weighted1")
                if L == 0:
                    def rest(n, h, q, i, first):
                        v = vals[:, q, :, 0:D + 2 * H]
                        pool.wait_ge(sem("part0_0"), n + 1)
                        pool.tensor_tensor(v, v, parts[q][:, 0, :, 0:D + 2 * H], ALU.subtract).then_inc(sem("rest0"), 1)

                    ring_steps(pool, rest)
            for j in range(XB):
                pool.wait_ge(sem(f"rel_stored{j}"), 16 * XI)
            gather(2, rel_rows[:, :], D, "acc2")

            def scatter_messages(i, first):
                for h in range(2):
                    hold(pool, "msg_made", 2 * GPH * i + GPH * h + GPH)
                    for t in range(HALF):
                        pool.indirect_dma_start(
                            out=messages[:, :], out_offset=bass.IndirectOffsetOnAxis(ap=idx_ring[:, h, t:t + 1], axis=0),
                            in_=ring[:, h, t, 0:MW], in_offset=None,
                            bounds_check=last_row, oob_is_err=False).then_inc(sem(f"msg_scattered{h}"), 16)

            pool.wait_ge(sem("msg_filled"), 16 * (T // HALF))
            loop(pool, RINGS, scatter_messages)

        cnt, ntf, incl, base = (small[:, j, 0:NB] for j in range(4))
        mi = msk.bitcast(i32)

        def rank_bases(dve, tag):
            before, total = bank(7, 0, NB), bank(7, 32, 32 + NB)
            nc.vector.memset(zrow, 0.0)
            nc.vector.memset(posf, POS_PAD)
            dve.wait_ge(sem(f"{tag}_summed"), 1)
            nc.vector.tensor_scalar(small_i[:, 0, 0:NB], total, float(P - 1), None, ALU.add)
            dve.drain()
            nc.vector.tensor_scalar(small_i[:, 1, 0:NB], small_i[:, 0, 0:NB], 7, None, ALU.logical_shift_right)
            dve.drain()
            nc.vector.tensor_copy(ntf, small_i[:, 1, 0:NB])
            dve.drain()
            nc.vector.tensor_tensor_scan(incl, ntf, zrow[:, 0:NB], 0.0, ALU.add, ALU.add)
            dve.drain()
            nc.vector.tensor_tensor(base, incl, ntf, ALU.subtract)
            nc.vector.tensor_tensor(blk_w[:, :, :], tval[:, :].unsqueeze(2).to_broadcast([P, TG, NB - 1]),
                                    incl[:, 0:NB - 1].unsqueeze(1).to_broadcast([P, TG, NB - 1]), ALU.is_ge)
            dve.drain()
            nc.vector.scalar_tensor_tensor(base, base, float(P), before, ALU.mult, ALU.add)
            nc.vector.tensor_reduce(blk_f, blk_w[:, :, :], AX.X, ALU.add)
            dve.drain()
            nc.vector.tensor_scalar(base, base, -1.0, None, ALU.add)
            nc.vector.tensor_copy(blk_i[:, :], blk_f).then_inc(sem("blk_made"), 1)
            dve.drain()

        def rank_bin(dve, b, start, j):
            nc.vector.tensor_scalar(mi[:, j, :], key, b, None, ALU.is_equal)
            dve.drain()
            nc.vector.tensor_tensor_scan(scn[:, j, :], mi[:, j, :], zrow, start, ALU.add, ALU.add)
            dve.drain()
            nc.vector.copy_predicated(posf, mi[:, j, :], scn[:, j, :])
            dve.drain()

        def rank_rows(dve):
            nc.vector.tensor_copy(mi[:, 0, :], posf)
            dve.drain()
            nc.vector.tensor_scalar(mi[:, 1, :], mi[:, 0, :], P - 1, None, ALU.bitwise_and)
            nc.vector.tensor_scalar(scn[:, 0, :].bitcast(i32), mi[:, 0, :], 7, None, ALU.logical_shift_right)
            dve.drain()
            nc.vector.scalar_tensor_tensor(row_of[:, :], mi[:, 1, :], float(T), scn[:, 0, :].bitcast(i32), ALU.mult, ALU.add)
            dve.drain()

        @block.vector
        def _(dve):
            nc.vector.memset(zeros[:, :], 0.0)
            dve.wait_ge(sem("iota"), 2)
            nc.vector.tensor_copy(iota_b[:, :], iota[:, :])
            dve.wait_ge(sem("masks"), 4)
            nc.vector.tensor_copy(ident_b[:, :], ident[:, :])
            nc.vector.tensor_scalar(far_id[:, :, :], ident[:, :].unsqueeze(1).to_broadcast([P, H, P]), -BIG, None, ALU.mult)
            nc.vector.tensor_tensor(small[:, 6, 0:GT * H], ident[:, 0:GT * H], ident[:, GT * H:2 * GT * H], ALU.add)
            dve.drain()
            nc.vector.tensor_tensor(small[:, 6, 0:GT * H], small[:, 6, 0:GT * H], ident[:, 2 * GT * H:3 * GT * H], ALU.add)
            nc.vector.memset(apart[:, :, :], 0.0)
            dve.drain()
            nc.vector.tensor_copy(pick, small[:, 6, 0:GT * H].unsqueeze(2).to_broadcast([P, GT * H, P]))
            nc.vector.memset(w24[:, :], 0.0).then_inc(sem("w24_cleared"), 1)
            nc.vector.memset(msg_pat, 0.0)
            dve.drain()
            nc.vector.memset(msg_pat[:, :, D:MW], -1.0).then_inc(sem("msg_pat_made"), 1)
            dve.wait_ge(sem("raw_loaded"), 16 * 2 * len(IN_F))
            r = raw.bitcast(i32)
            s_i, d_i, t8_i, t24_i = (r[:, j, :] for j in range(4))
            lo_i, hi_i = msk[:, 0, :].bitcast(i32), msk[:, 1, :].bitcast(i32)
            nc.vector.tensor_copy(rec[:, :, F_SRC], s_i)
            nc.vector.scalar_tensor_tensor(rec[:, :, F_ROW], t8_i, float(NPAD), s_i, ALU.mult, ALU.add)
            nc.vector.tensor_copy(rec[:, :, F_T24], t24_i)
            nc.vector.tensor_copy(rec[:, :, F_NORM], raw[:, 4, :])
            nc.vector.tensor_scalar(lo_i, s_i, P - 1, None, ALU.bitwise_and)
            nc.vector.tensor_scalar(hi_i, s_i, 7, None, ALU.logical_shift_right)
            dve.drain()
            nc.vector.tensor_copy(rec[:, :, F_SLO], lo_i)
            nc.vector.tensor_copy(rec[:, :, F_SHI], hi_i)
            dve.drain()
            nc.vector.tensor_scalar(lo_i, d_i, P - 1, None, ALU.bitwise_and)
            nc.vector.tensor_scalar(hi_i, d_i, 7, None, ALU.logical_shift_right)
            nc.vector.memset(rec[:, :, F_NORM + 1:F_NORM + 2], 0.0)
            dve.drain()
            nc.vector.tensor_copy(rec[:, :, F_DLOC], lo_i)
            nc.vector.tensor_copy(key, hi_i)
            dve.drain()
            for b in range(NB):
                if b % 2 == 0:
                    dve.drain()
                nc.vector.tensor_scalar(msk[:, b % 2, :], key, float(b), None, ALU.is_equal, ALU.add,
                                        accum_out=cnt[:, b:b + 1])
            nc.vector.memset(small[:, 3, NB:NB + 4], 0.0).then_inc(sem("dst_counted"), 1)
            rank_bases(dve, "dst")
            for b in range(NB + 2):
                if b >= 2:
                    nc.vector.copy_predicated(posf, mi[:, b % 2, :], scn[:, b % 2, :])
                    dve.drain()
                if b < NB:
                    nc.vector.tensor_scalar(mi[:, b % 2, :], key, float(b), None, ALU.is_equal)
                if 1 <= b <= NB:
                    a = b - 1
                    nc.vector.tensor_tensor_scan(scn[:, a % 2, :], mi[:, a % 2, :], zrow, base[:, a:a + 1], ALU.add, ALU.add)
                dve.drain()
            rank_rows(dve)

            def stage_records(i, first):
                for h in range(2):
                    k = 2 * i + h
                    if not first:
                        dve.wait_ge(sem(f"rec_scattered{h}"), 16 * HALF * i)
                    elif h == 0:
                        dve.wait_ge(sem("rec_filled"), 16 * (T // HALF))
                    t0 = bass.ds(k * HALF, HALF)
                    nc.vector.tensor_copy(rec_ring(h)[:, :, 0:8], rec[:, t0, 0:8])
                    nc.vector.tensor_copy(idx_ring[:, h, :], row_of[:, t0])
                    dve.wait_ge(sem("eatt_quad"), 2 * k + 2)
                    nc.vector.tensor_copy(rec_ring(h)[:, :, F_EATT:F_EATT + H],
                                          bank(2 + h, 0, HALF * H).rearrange("p (t h) -> p t h", h=H)).then_inc(sem("rec_staged"), 1)

            loop(dve, RINGS, stage_records)

            def split(f, parts):
                nc.vector.tensor_copy(parts[0], f)
                dve.drain()
                nc.vector.tensor_tensor(f, f, parts[0], ALU.subtract)
                dve.drain()
                nc.vector.tensor_copy(parts[1], f)
                dve.drain()
                nc.vector.tensor_tensor(parts[2], f, parts[1], ALU.subtract)
                dve.drain()

            def projected(L):
                def body(i, first):
                    hold(dve, f"proj_mm{L}", i + 1)
                    for c0, nb, bk in ((0, 3, 2), (3, 2, 3)):
                        v = bank(bk, 0, nb * PC).rearrange("p (b c) -> p b c", c=PC)
                        b0 = bass.ds(XB * i + c0, nb)
                        nc.vector.tensor_copy(rows_sb[:, b0, :], v[:, :, 0:RW])
                        last = nc.vector.tensor_copy(tab_f[:, :, :].rearrange("p h b -> p b h")[:, b0, :], v[:, :, RW:RW + H])
                    last.then_inc(sem(f"projected{L}"), 1)
                loop(dve, XI, body)
                dve.wait_ge(sem("blk_spread"), 16)
                nc.vector.tensor_scalar(blk_hot, blk_all, tval[:, 0:1], None, ALU.is_equal).then_inc(sem(f"blk_hot{L}"), 1)
                for j in range(2 * H):
                    dve.wait_ge(sem(f"tab_mm{L}"), j + 1)
                    nc.vector.tensor_copy(tab_w[:, (j % 2) * MID:(j % 2) * MID + MID, j // 2], bank(j, 0, MID))
                dve.drain()
                split(tab_w, [tab_t[:, :, k, :] for k in range(3)])
                nc.vector.memset(small[:, 11, 0:1], 0.0).then_inc(sem("tab_split"), 1)

            def scores():
                def term(n, h, q, i, early):
                    p = q % 2
                    if q == 0:
                        dve.wait_ge(sem(f"gathered0_{h}"), 16 * HALF * i + 16 * HALF)
                    src_terms = ring[:, h, q * GT:q * GT + GT, D:RW]
                    tgt_terms = bank(2 + p, 0, GT * H).rearrange("p (t h) -> p t h", h=H)
                    nc.vector.tensor_tensor(pre_g[:, p, :, :], rec[:, bass.ds(n * GT, GT), F_EATT:F_EATT + H], src_terms, ALU.add)
                    dve.drain()
                    if not early:
                        dve.wait_ge(sem("att_kept"), n - 1)
                    dve.wait_ge(sem("looked0"), n + 1)
                    W = GT * H
                    rest = pre_g[:, p, :, :].rearrange("p t h -> p (t h)")
                    part = [apart[:, p, k * W:k * W + W] for k in range(3)]
                    nc.vector.tensor_tensor(att_g[:, p, :].rearrange("p (t h) -> p t h", h=H), tgt_terms, pre_g[:, p, :, :], ALU.add)
                    nc.vector.tensor_tensor(part[0].rearrange("p (t h) -> p t h", h=H), tgt_terms, pre_g[:, p, :, :], ALU.add)
                    dve.drain()
                    nc.vector.tensor_tensor(rest, att_g[:, p, :], part[0], ALU.subtract)
                    nc.vector.tensor_tensor(part[1], att_g[:, p, :], part[0], ALU.subtract)
                    dve.drain()
                    nc.vector.tensor_tensor(part[2], rest, part[1], ALU.subtract).then_inc(sem("scored0"), 1)

                def largest(n):
                    for c in range(2):
                        hold(dve, "spread", 2 * n + c + 1)
                        nc.vector.tensor_reduce(att2[:, bass.ds(n * GT + 2 * c, 2), :],
                                                PS[:, (4 + 2 * c) * BK:(6 + 2 * c) * BK].rearrange("p (t h e) -> p t h e", h=H, e=P),
                                                AX.X, ALU.max).then_inc(sem("maxed"), 1)

                def hot(n, q, early):
                    if not early:
                        dve.wait_ge(sem("spread"), 2 * n - 6)
                    nc.vector.tensor_tensor(
                        hot4(q).rearrange("p (t c) -> p t c", c=P), iota_b[:, :].unsqueeze(1).to_broadcast([P, GT, P]),
                        rec[:, bass.ds(n * GT, GT), F_DLOC:F_DLOC + 1].to_broadcast([P, GT, P]), ALU.not_equal).then_inc(sem("hot_made"), 1)

                def body0(n, h, q, i, first, last_pass):
                    start = first and h == 0
                    if not (last_pass and h and q == GPH - 1):
                        hot(n + 1, (q + 1) % GPH, start and q < GPH - 1)
                    if not (start and q == 0):
                        term(n - 1, *before(h, q), i, start and q < 3)
                    if not (start and q < 2):
                        largest(n - 2)

                hot(0, 0, True)
                ring_steps(dve, body0, peel_last=True)
                term(LASTG, 1, GPH - 1, RINGS - 1, False)
                largest(LASTG - 1)
                largest(LASTG)
                dve.wait_ge(sem("att_kept"), T // GT)
                maxima()
                dve.drain()
                nc.vector.tensor_scalar(att2[:, :, 0:1], rec[:, :, F_DLOC:F_DLOC + 1], 0.0, -HUGE, ALU.is_lt, ALU.mult)
                nc.vector.scalar_tensor_tensor(att, att, 0.2, att, ALU.mult, ALU.max)
                dve.drain()
                nc.vector.tensor_tensor(att, att, att2[:, :, 0:1].to_broadcast([P, T, H]), ALU.add)
                dve.drain()

            def maxima():
                nc.vector.memset(same[:, 0:1], 0.0)
                nc.vector.memset(same[:, T:T + 1], 0.0)
                nc.vector.tensor_tensor(same[:, 1:T], blk_all[:, 1:T], blk_all[:, 0:T - 1], ALU.is_equal)
                dve.drain()
                for h in range(H):
                    nc.vector.tensor_tensor_scan(back[:, ::-1], same[:, T:0:-1], att2[:, ::-1, h], 0.0, ALU.mult, ALU.max)
                    nc.vector.tensor_tensor_scan(tab_w[:, :, h], same[:, 0:T], att2[:, :, h], 0.0, ALU.mult, ALU.max)
                    dve.drain()
                    nc.vector.tensor_tensor(tab_w[:, :, h], tab_w[:, :, h], back, ALU.max)
                    dve.drain()
                dve.drain()
                split(tab_w, [tab_t[:, :, k, :] for k in range(3)])
                for a in parts:
                    nc.vector.memset(a[:, 0, :, VW - 1:VW], 1.0)
                nc.vector.memset(small[:, 11, 2:3], 0.0).then_inc(sem("tab_split"), 1)

            def norms_and_ranking(weigh_norms):
                bins, vals_j = small[:, 9, :], small[:, 10, :]

                def count_two(i):
                    nc.vector.tensor_copy(bins[:, 0:2], iota[:, bass.ds((i - 2) * 2, 2)])
                    dve.drain()
                    for j in range(2):
                        nc.vector.tensor_scalar(msk[:, j, :], key, bins[:, j:j + 1], None, ALU.is_equal, ALU.add,
                                                accum_out=vals_j[:, j:j + 1])
                    dve.drain()
                    nc.vector.tensor_copy(small[:, 0, bass.ds((i - 2) * 2, 2)], vals_j[:, 0:2])

                def step(i, first, extra=None):
                    for h in range(2):
                        for q in range(GPH):
                            if extra and (h, q) in ((0, 1), (0, 3), (1, 2)):
                                extra(i, {(0, 1): 0, (0, 3): 1, (1, 2): 2}[h, q])
                            weigh_norms(2 * GPH * i + GPH * h + q, h, q, i, first)

                def count(i, j):
                    if j == 0:
                        count_two(i)

                def position(i, j):
                    if j == 0:
                        nc.vector.tensor_copy(bins[:, 0:3], iota[:, bass.ds((i - POS_AT) * 3, 3)])
                        nc.vector.tensor_copy(vals_j[:, 0:3], small[:, 3, bass.ds((i - POS_AT) * 3, 3)])
                        dve.drain()
                    rank_bin(dve, bins[:, j:j + 1], vals_j[:, j:j + 1], j % 2)

                step(0, True)
                step(1, False)
                with dve.Fori(2, SUM_AT) as i:
                    step(i, False, count)
                dve.drain()
                nc.vector.memset(small[:, 11, 3:4], 0.0).then_inc(sem("src_counted"), 1)
                step(SUM_AT, False)
                rank_bases(dve, "src")
                with dve.Fori(POS_AT, ROWS_AT) as i:
                    step(i, False, position)
                rank_rows(dve)
                with dve.Fori(ROWS_AT, RINGS) as i:
                    step(i, False)

            def weigh(L):
                w = D + (2 * H if L == 0 else H)

                def scale(n, h, q, i):
                    if q == 0 and L == 0:
                        dve.wait_ge(sem(f"rows_loaded0_{h}"), 16 * i + 16)
                    dve.wait_ge(sem(f"weights_made{L}"), n + 1)
                    nc.vector.tensor_tensor(
                        vals[:, q, :, 0:D].rearrange("p t (h c) -> p t h c", h=H),
                        ring[:, h, q * GT:q * GT + GT, 0:D].rearrange("p t (h c) -> p t h c", h=H),
                        vals[:, q, :, D:D + H].unsqueeze(3).to_broadcast([P, GT, H, HD]), ALU.mult).then_inc(sem(f"weighted{L}"), 1)

                def rest(n, q):
                    dve.wait_ge(sem(f"part0_{L}"), n + 1)
                    nc.vector.tensor_tensor(vals[:, q, :, 0:w], vals[:, q, :, 0:w], parts[q][:, 0, :, 0:w], ALU.subtract).then_inc(sem(f"rest{L}"), 1)

                def last_part(n, q, early):
                    dve.wait_ge(sem(f"part1_{L}"), n + 1)
                    nc.vector.tensor_tensor(parts[q][:, 2, :, 0:w], vals[:, q, :, 0:w], parts[q][:, 1, :, 0:w], ALU.subtract)
                    if not early:
                        dve.wait_ge(sem(f"acc{L}"), n - 3)
                    nc.vector.tensor_tensor(
                        hot4(q).rearrange("p (t c) -> p t c", c=P), iota_b[:, :].unsqueeze(1).to_broadcast([P, GT, P]),
                        rec[:, bass.ds(n * GT, GT), F_DLOC:F_DLOC + 1].to_broadcast([P, GT, P]), ALU.is_equal).then_inc(sem(f"parts_made{L}"), 1)

                def body(n, h, q, i, first):
                    start = first and h == 0
                    if L == 0:
                        dve.wait_ge(sem("looked_m"), n + 1)
                        nc.vector.tensor_tensor(arg_g[:, q % 2, :, :], att[:, bass.ds(n * GT, GT), :],
                                                bank(7, 0, GT * H).rearrange("p (t h) -> p t h", h=H),
                                                ALU.subtract).then_inc(sem("shifted"), 1)
                    if not (start and q < 1):
                        scale(n - 1, *before(h, q), i)
                    if not (start and q < 3):
                        last_part(n - 3, before(h, q, 3)[1], first and GPH * h + q < 7)

                def weigh_norms(n, h, q, i, first):
                    if not (first and h == 0 and q < 2):
                        dve.wait_ge(sem("acc2"), n - 1)
                    for t in range(GT):
                        e = bass.ds(n * GT + t, 1)
                        last = nc.vector.tensor_scalar(ohf[:, q % 2, t, :], iota[:, :], rec[:, e, F_DLOC],
                                                       rec[:, e, F_NORM], ALU.is_equal, ALU.mult)
                    last.then_inc(sem("weighted2"), 1)

                def half_scores(m, h, i):
                    a, pad = att_h[:, h, :, :], small[:, 6 + h, 0:HALF]
                    nc.vector.tensor_scalar(pad, rec[:, bass.ds(m * HALF, HALF), F_DLOC], 0.0, -HUGE, ALU.is_lt, ALU.mult)
                    dve.wait_ge(sem("looked1"), GPH * m + GPH)
                    dve.wait_ge(sem(f"gathered1_{h}"), 16 * HALF * i + 16 * HALF)
                    nc.vector.tensor_tensor(a, bank(7, 0, HALF * H).rearrange("p (t h) -> p t h", h=H), ring[:, h, :, D:RW], ALU.add)
                    dve.drain()
                    nc.vector.scalar_tensor_tensor(a, a, 0.2, a, ALU.mult, ALU.max)
                    dve.drain()
                    nc.vector.tensor_tensor(a, a, pad.unsqueeze(2).to_broadcast([P, HALF, H]), ALU.add)
                    dve.drain()
                    nc.vector.tensor_reduce(small[:, 5, 0:1], a, AX.XY, ALU.max).then_inc(sem("lane_max"), 1)

                def over_lanes(m):
                    dve.wait_ge(sem("lane_max_turned"), m + 1)
                    nc.vector.tensor_reduce(small[0:1, 5, 1:2], bank(7, P, 2 * P)[0:1, :], AX.X, ALU.max).then_inc(sem("one_max"), 1)

                def running_max(m):
                    old, new, step, neg = (small[:, 5, j:j + 1] for j in (3, 6, 4, 2))
                    dve.wait_ge(sem("max_spread"), m + 1)
                    nc.vector.tensor_tensor(new, bank(7, 3 * P, 3 * P + 1), old, ALU.max)
                    dve.drain()
                    nc.vector.tensor_tensor(step, old, new, ALU.subtract)
                    nc.vector.tensor_scalar(neg, new, -1.0, None, ALU.mult)
                    dve.drain()
                    nc.vector.tensor_copy(old, new).then_inc(sem("max_ready"), 1)

                def rescale(m):
                    dve.wait_ge(sem("factor_made"), m + 1)
                    dve.wait_ge(sem("acc1"), GPH * m)
                    nc.vector.tensor_scalar(PS[:, 0:CUT], PS[:, 0:CUT], small[:, 5, 5:6], None, ALU.mult).then_inc(sem("rescaled_v"), 1)

                def half_body(i, first):
                    for h in range(2):
                        m, start = 2 * i + h, first and h == 0
                        n = GPH * m
                        half_scores(m, h, i)
                        if not start:
                            rest(n - 1, 3)
                        over_lanes(m)
                        if not start:
                            last_part(n - 1, 3, first)
                        running_max(m)
                        scale(n, h, 0, i)
                        scale(n + 1, h, 1, i)
                        rest(n, 0)
                        if not start:
                            rescale(m)
                        last_part(n, 0, start)
                        rest(n + 1, 1)
                        scale(n + 2, h, 2, i)
                        last_part(n + 1, 1, start)
                        rest(n + 2, 2)
                        scale(n + 3, h, 3, i)
                        last_part(n + 2, 2, start)

                if L == 2:
                    norms_and_ranking(weigh_norms)
                    return
                if L == 1:
                    nc.vector.memset(small[:, 5, 3:4], -HUGE)
                    dve.drain()
                    loop(dve, RINGS, half_body)
                    rest(LASTG, GPH - 1)
                    last_part(LASTG, GPH - 1, False)
                    return
                ring_steps(dve, body)
                scale(LASTG, 1, GPH - 1, RINGS - 1)
                for k in range(2, -1, -1):
                    last_part(LASTG - k, GPH - 1 - k, False)

            def norm(L):
                acc = PS[:, 0:NB * D]
                acc3 = acc.rearrange("p (b c) -> p b c", c=D)
                y = h_sb
                dve.wait_ge(sem(f"acc{L}"), T // GT)
                if L < 2:
                    sums, den, edg = stat[:, 0, :], stat[:, 1, 0:NB * H], stat[:, 6, 0:NB]
                    s3 = sums.rearrange("p (b s) -> p b s", s=NS)
                    d3 = den.rearrange("p (b h) -> p b h", h=H)
                    nc.vector.tensor_copy(sums, PS[:, SUM0:SUM0 + NB * NS])
                    dve.drain()
                    if L == 0:
                        has = stat[:, 3, 0:NB]
                        nc.vector.tensor_scalar(edg, s3[:, :, NS - 1], -1.0, float(E), ALU.mult, ALU.add)
                        nc.vector.tensor_scalar(has, s3[:, :, NS - 1], 1.0, None, ALU.max)
                        dve.drain()
                        nc.vector.reciprocal(has, has)
                        dve.drain()
                        nc.vector.tensor_tensor(edg, edg, has, ALU.mult)
                        dve.drain()
                        nc.vector.tensor_tensor(d3, s3[:, :, H:2 * H], edg.unsqueeze(2).to_broadcast([P, NB, H]), ALU.mult)
                        nc.vector.tensor_scalar(has, s3[:, :, NS - 1], 0.0, None, ALU.is_equal)
                        dve.drain()
                        nc.vector.tensor_tensor(d3, d3, s3[:, :, 0:H], ALU.add)
                        dve.drain()
                        nc.vector.tensor_tensor(d3, d3, has.unsqueeze(2).to_broadcast([P, NB, H]), ALU.add)
                    else:
                        nc.vector.tensor_scalar(d3, s3[:, :, 0:H], 1e-16, None, ALU.add)
                    dve.drain()
                    nc.vector.reciprocal(den, den)
                    dve.drain()
                    nc.vector.tensor_tensor(y.rearrange("p b (h c) -> p (b h) c", h=H), acc.rearrange("p (g c) -> p g c", c=HD),
                                            den.unsqueeze(2).to_broadcast([P, NB * H, HD]), ALU.mult)
                    dve.drain()
                    nc.vector.tensor_tensor(y, y, xs[:, :, :], ALU.add)
                    dve.drain()
                elif L == 2:
                    nc.vector.scalar_tensor_tensor(y, acc3, 0.0, xs[:, :, :], ALU.max, ALU.add)
                    dve.drain()
                else:
                    nc.vector.tensor_tensor(y, acc3, xs[:, :, :], ALU.add)
                    dve.drain()
                tot, var = stat[:, 4, 0:NB], stat[:, 5, 0:NB]
                nc.vector.tensor_reduce(tot, y, AX.X, ALU.add)
                dve.drain()
                nc.vector.tensor_scalar(tot, tot, 1.0 / D, None, ALU.mult)
                dve.drain()
                nc.vector.tensor_tensor(y, y, tot.unsqueeze(2).to_broadcast([P, NB, D]), ALU.subtract)
                dve.drain()
                sq = arena[:, 0:NB * D].rearrange("p (b c) -> p b c", c=D)
                nc.vector.tensor_tensor(sq, y, y, ALU.mult)
                dve.drain()
                nc.vector.tensor_reduce(var, sq, AX.X, ALU.add)
                dve.drain()
                nc.vector.tensor_scalar(var, var, 1.0 / D, EPS, ALU.mult, ALU.add).then_inc(sem("var_made"), 1)
                dve.wait_ge(sem("std_made"), L + 1)
                nc.vector.reciprocal(stat[:, 7, 0:NB], stat[:, 6, 0:NB])
                dve.drain()
                nc.vector.tensor_tensor(xs[:, :, :], y, stat[:, 7, 0:NB].unsqueeze(2).to_broadcast([P, NB, D]), ALU.mult).then_inc(sem("normed"), 1)
                dve.drain()

            def relations():
                def body(i, first):
                    for j in range(XB):
                        n = XB * i + j
                        dve.wait_ge(sem("rel_mm"), n + 1)
                        if not first:
                            dve.wait_ge(sem(f"rel_stored{j}"), 16 * i)
                        nc.vector.tensor_tensor(rel_stage[:, j, :], PS[:, (2 + 2 * (j % 3)) * BK:(4 + 2 * (j % 3)) * BK],
                                                b_rel_bc, ALU.add).then_inc(sem("rel_made"), 1)
                dve.wait_ge(sem("rel_loaded"), 32)
                loop(dve, XI, body)

            def make_messages():
                def product(i, h, q):
                    n, p = 2 * GPH * i + GPH * h + q, q % 2
                    t0 = bass.ds(n * GT, GT)
                    dve.wait_ge(sem("rel_copied"), n + 1)
                    nc.vector.tensor_tensor(ring[:, h, q * GT:q * GT + GT, 0:D], bank(2 + p).rearrange("p (t c) -> p t c", c=D),
                                            scaled[:, p, :, :], ALU.mult)
                    nc.vector.tensor_copy(ring[:, h, q * GT:q * GT + GT, D:MW], rec[:, t0, F_SLO:F_SLO + 1]).then_inc(sem("msg_made"), 1)

                def hot(n, q, early):
                    if not early:
                        dve.wait_ge(sem("transposed_g"), n - 3)
                    nc.vector.tensor_tensor(
                        hot4(q).rearrange("p (t c) -> p t c", c=P), iota_b[:, :].unsqueeze(1).to_broadcast([P, GT, P]),
                        rec[:, bass.ds(n * GT, GT), F_T24:F_T24 + 1].to_broadcast([P, GT, P]), ALU.is_equal).then_inc(sem("one_hot_g"), 1)

                def body(n, h, q, i, first, last_pass):
                    if not (last_pass and h and q == GPH - 1):
                        hot(n + 1, (q + 1) % GPH, first and h == 0 and q < GPH - 1)
                    if q:
                        product(i, h, q - 1)
                    elif h:
                        product(i, 0, GPH - 1)
                    elif not first:
                        product(i - 1, 1, GPH - 1)
                    if q == 0:
                        if not first:
                            dve.wait_ge(sem(f"msg_scattered{h}"), 16 * HALF * i)
                        nc.vector.tensor_copy(idx_ring[:, h, :], row_of[:, bass.ds((2 * i + h) * HALF, HALF)])

                hot(0, 0, True)
                ring_steps(dve, body, peel_last=True)
                product(RINGS - 1, 1, GPH - 1)

            def source_hot():
                def body(i, first):
                    for h in range(2):
                        for q in range(GPH):
                            n, p = 2 * GPH * i + GPH * h + q, q % 2
                            if q == 0:
                                dve.wait_ge(sem(f"msg_loaded{h}"), 16 * i + 16)
                            if not (first and h == 0 and q < 2):
                                dve.wait_ge(sem("acc3"), n - 1)
                            nc.vector.tensor_tensor(ohf[:, p, :, :], iota[:, :].unsqueeze(1).to_broadcast([P, GT, P]),
                                                    ring[:, h, q * GT:q * GT + GT, D:MW].to_broadcast([P, GT, P]),
                                                    ALU.is_equal).then_inc(sem("weighted3"), 1)
                loop(dve, RINGS, body)

            projected(0)
            dve.wait_ge(sem("rec_loaded"), 16)
            dve.wait_ge(sem("msg_filled"), 16 * (T // HALF))
            dve.wait_ge(sem("rows_stored0"), 16)
            scores()
            weigh(0)
            norm(0)
            projected(1)
            dve.wait_ge(sem("rows_stored1"), 16)
            nc.vector.tensor_tensor(xs[:, :, :], xs[:, :, :], bias_bc[:, :].unsqueeze(1).to_broadcast([P, NB, D]), ALU.add)
            weigh(1)
            norm(1)
            relations()
            for j in range(XB):
                dve.wait_ge(sem(f"rel_stored{j}"), 16 * XI)
            nc.vector.tensor_scalar(zrow, rec[:, :, F_DLOC], 0.0, float(2 * NB), ALU.is_lt, ALU.mult)
            dve.drain()
            nc.vector.tensor_tensor(key, zrow, rec[:, :, F_SHI], ALU.add)
            dve.drain()
            dve.wait_ge(sem("w24_loaded"), 16)
            nc.vector.tensor_copy(w24f[:, :], w24[:, :])
            dve.drain()
            split(w24f[:, :], [w24s[:, k, :] for k in range(3)])
            weigh(2)
            norm(2)
            rest, x2 = h_sb.rearrange("p b c -> p (b c)"), xs[:, :, :].rearrange("p b c -> p (b c)")
            nc.vector.tensor_copy(xs3[:, 0, :], x2)
            dve.drain()
            nc.vector.tensor_tensor(rest, x2, xs3[:, 0, :], ALU.subtract)
            dve.drain()
            nc.vector.tensor_copy(xs3[:, 1, :], rest)
            dve.drain()
            nc.vector.tensor_tensor(xs3[:, 2, :], rest, xs3[:, 1, :], ALU.subtract).then_inc(sem("x_split"), 1)
            make_messages()
            source_hot()
            norm(3)

        @block.scalar
        def _(act):
            for h in range(H):
                act.dma_start(acol[HD * h:HD * h + HD, 0:3], att_a[h, :].rearrange("(j d) -> d j", j=3)).then_inc(sem("par_loaded"), 16)
            act.dma_start(acol[:, 3:4], att_src.rearrange("o h d -> (h d) o")).then_inc(sem("par_loaded"), 16)
            act.dma_start(acol[:, 4:5], att_tgt.rearrange("o h d -> (h d) o")).then_inc(sem("par_loaded"), 16)
            act.dma_start(w_nat[:, :], W_node).then_inc(sem("par_loaded"), 16)
            act.dma_start(we2[:, 0:KE], W_edge).then_inc(sem("par_loaded"), 16)
            act.dma_start(we2[:, KE:2 * KE], W_edge).then_inc(sem("par_loaded"), 16)
            act.dma_start(wx[:, 1, 0:D], W_proj).then_inc(sem("par_loaded"), 16)
            act.dma_start(bias_bc[:, :], proj_bias.rearrange("(o c) -> o c", o=1).to_broadcast([P, D])).then_inc(sem("par_loaded"), 16)
            act.wait_ge(sem("par_loaded"), 16 * (H + 7))
            act.wait_ge(sem("masks"), 4)
            for j in range(5):
                act.activation(aexp[:, j, :], headmask[:, :], ACT.Copy, scale=acol[:, j:j + 1])
            act.activation(wea2[:, :, :], headmask[:, :].unsqueeze(1).to_broadcast([P, 2, H]), ACT.Copy, scale=0.0)\
                .then_inc(sem("aexp"), 1)
            act.drain()
            act.wait_ge(sem("wT_made"), 1)
            act.activation(wx[:, 0, 0:D], bank(0, 0, D), ACT.Copy)
            act.activation(wpT[:, :], bank(0, D, 2 * D), ACT.Copy).then_inc(sem("wpT"), 1)
            act.wait_ge(sem("wa_made"), 1)
            act.activation(wx[:, 0, D:D + 2 * H], bank(1, 0, 2 * H), ACT.Copy)
            act.activation(wx[:, 1, D:D + 2 * H], bank(1, 32, 32 + 2 * H), ACT.Copy)
            act.activation(wea2[0:KE, 0, :], bank(1, 64, 64 + H)[0:KE, :], ACT.Copy)
            act.activation(wea2[KE:2 * KE, 1, :], bank(1, 64, 64 + H)[KE:2 * KE, :], ACT.Copy).then_inc(sem("wx_made"), 1)

            act.wait_ge(sem("w24_cleared"), 1)
            act.dma_start(w24[0:R24, :], rel_weight).then_inc(sem("w24_loaded"), 16)
            act.wait_ge(sem("msg_pat_made"), 1)

            def attr_copy(i, first):
                for h in range(2):
                    act.dma_start(msg_v[:, bass.ds((2 * i + h) * HALF, HALF), :], msg_pat).then_inc(sem("msg_filled"), 16)
                    for q in range(2):
                        n = 4 * i + 2 * h + q
                        act.wait_ge(sem("attr_transposed"), n + 1)
                        if not first or h:
                            act.wait_ge(sem("eatt_quad"), n - 1)
                        act.activation(scaled[:, q, :, :].rearrange("p g c -> p (g c)"), bank(q), ACT.Copy).then_inc(sem("attrT"), 1)

            loop(act, RINGS, attr_copy)

            def turn_nodes(L):
                def body(i, first):
                    if not first:
                        hold(act, f"x_turned{L}", i)
                    act.activation(x_stage, xs[:, bass.ds(XB * i, XB), :].rearrange("p b c -> p (b c)"), ACT.Copy).then_inc(sem(f"x_staged{L}"), 1)
                    hold(act, f"x_turned{L}", i + 1)
                    if not first:
                        act.wait_ge(sem(f"proj_mm{L}" if L < 2 else "rel_mm"), i if L < 2 else XB * i)
                    act.activation(xT, PS[:, 0:XB * P], ACT.Copy).then_inc(sem(f"xT{L}"), 1)
                loop(act, XI, body)

            def stage_idx(L, i, h, field, first):
                if not first:
                    hold(act, f"gathered{L}_{h}", 16 * HALF * i)
                act.activation(idx_ring[:, h, :], rec[:, bass.ds((2 * i + h) * HALF, HALF), field], ACT.Copy).then_inc(sem(f"idx_staged{L}"), 1)

            def stage_all_idx(L, field):
                with act.Fori(1, RINGS) as i:
                    for h in range(2):
                        stage_idx(L, i, h, field, False)

            def spread_table(L):
                act.wait_ge(sem(f"tab_turned{L}"), 1)
                act.activation(tab_T[0:NB, :], bank(6)[0:NB, :], ACT.Copy).then_inc(sem(f"tab_T{L}"), 1)

            def table_half(tag, looked, i, h, first):
                if not first:
                    hold(act, looked, 2 * GPH * i + GPH * h - GPH)
                act.activation(tab_h[:, h, :, :, :], tab_t[:, bass.ds((2 * i + h) * HALF, HALF), :, :], ACT.Copy).then_inc(sem(f"tab_half_{tag}"), 1)

            def gather_loop(L):
                def keep(n, p):
                    act.wait_ge(sem("parts_turned"), n + 1)
                    act.activation(apartT[0:KP, p, :], bank(2 + p, 64, 128).bitcast(bf16)[0:KP, :], ACT.Copy).then_inc(sem("partsT"), 1)
                    hold(act, "scored0", n + 1)
                    act.activation(att[:, bass.ds(n * GT, GT), :], att_g[:, p, :].rearrange("p (t h) -> p t h", h=H), ACT.Copy).then_inc(sem("att_kept"), 1)

                def step(i, first, last=False):
                    for h in range(2):
                        if h == 0 and not first:
                            stage_idx(L, i, 1, F_SRC, False)
                        elif h == 1 and not last:
                            stage_idx(L, i + 1, 0, F_SRC, False)
                        if L == 0:
                            table_half("t0", "looked0", i, h, first)
                        elif h == 0:
                            table_half("t1", "looked1", i, 1, first)
                        elif not last:
                            table_half("t1", "looked1", i + 1, 0, False)
                        if L == 1:
                            weigh_half(2 * i + h, h, first and h == 0)
                            continue
                        for q in range(GPH):
                            n, p = 2 * GPH * i + GPH * h + q, q % 2
                            act.wait_ge(sem("turned"), n + 1)
                            if q == 0 and not first:
                                act.wait_ge(sem(f"hotT_saved_{h}"), 16 * i)
                            act.activation(hotT[:, h, q * GT * P:(q + 1) * GT * P], bank(p).bitcast(bf16)[:, 0:GT * P],
                                           ACT.Copy, scale=-1.0, bias=1.0).then_inc(sem("hotT_made"), 1)
                            if not (first and h == 0 and q == 0):
                                keep(n - 1, 1 - p)

                act.wait_ge(sem("tab_split"), 1 + 2 * L)
                if L == 1:
                    table_half("t1", "looked1", 0, 0, True)
                step(0, True)
                step(1, False)
                with act.Fori(2, RINGS - 1) as i:
                    step(i, False)
                step(RINGS - 1, False, True)
                if L == 0:
                    keep(LASTG, 1)
                else:
                    part1(1, LASTG, GPH - 1)

            def part0(L, n, q, early):
                w = D + (2 * H if L == 0 else H)
                act.wait_ge(sem(f"weighted{L}"), n + 1)
                if not early:
                    act.wait_ge(sem(f"acc{L}"), n - 3)
                act.activation(parts[q][:, 0, :, 0:w], vals[:, q, :, 0:w], ACT.Copy).then_inc(sem(f"part0_{L}"), 1)

            def part1(L, n, q):
                w = D + (2 * H if L == 0 else H)
                act.wait_ge(sem(f"rest{L}"), n + 1)
                act.activation(parts[q][:, 1, :, 0:w], vals[:, q, :, 0:w], ACT.Copy).then_inc(sem(f"part1_{L}"), 1)

            def weigh_half(m, h, start):
                n = GPH * m
                if not start:
                    part1(1, n - 1, GPH - 1)
                act.wait_ge(sem("max_ready"), m + 1)
                act.activation(small[:, 5, 5:6], small[:, 5, 4:5], ACT.Exp).then_inc(sem("factor_made"), 1)
                for q in range(GPH):
                    if not start:
                        act.wait_ge(sem("parts_made1"), n + q - 3)
                    act.activation(vals[:, q, :, D:D + H], att_h[:, h, q * GT:q * GT + GT, :], ACT.Exp, bias=small[:, 5, 2:3])\
                        .then_inc(sem("weights_made1"), 1)
                part0(1, n, 0, start)
                part0(1, n + 1, 1, start)
                part1(1, n, 0)
                if not start:
                    act.wait_ge(sem("acc1"), n)
                    act.activation(PS[:, CUT:SUM0 + NB * NS], PS[:, CUT:SUM0 + NB * NS], ACT.Copy, scale=small[:, 5, 5:6])\
                        .then_inc(sem("rescaled_a"), 1)
                part1(1, n + 1, 1)
                part0(1, n + 2, 2, start)
                part1(1, n + 2, 2)
                part0(1, n + 3, 3, start)

            def weights():
                def body(n, h, q, i, first):
                    start = first and h == 0
                    if q == 0:
                        table_half("m", "looked_m", i, h, first)
                    if not start:
                        act.wait_ge(sem("parts_made0"), n - 3)
                    act.wait_ge(sem("shifted"), n + 1)
                    act.activation(vals[:, q, :, D:D + H], arg_g[:, q % 2, :, :], ACT.Exp)
                    act.activation(vals[:, q, :, D + H:D + 2 * H], bank(7, 0, GT * H).rearrange("p (t h) -> p t h", h=H),
                                   ACT.Exp, scale=-1.0).then_inc(sem("weights_made0"), 1)
                    if not (start and q < 1):
                        part0(0, n - 1, before(h, q)[1], first and GPH * h + q < 5)
                    if not (start and q < 2):
                        part1(0, n - 2, before(h, q, 2)[1])

                ring_steps(act, body)
                part0(0, LASTG, GPH - 1, False)
                part1(0, LASTG - 1, GPH - 2)
                part1(0, LASTG, GPH - 1)

            def std(L):
                act.wait_ge(sem("var_made"), L + 1)
                act.activation(stat[:, 6, 0:NB], stat[:, 5, 0:NB], ACT.Sqrt).then_inc(sem("std_made"), 1)

            turn_nodes(0)
            act.wait_ge(sem("rec_loaded"), 16)
            stage_idx(0, 0, 0, F_SRC, True)
            stage_idx(0, 0, 1, F_SRC, True)
            spread_table(0)
            act.wait_ge(sem("msg_filled"), 16 * (T // HALF))
            gather_loop(0)
            act.wait_ge(sem("tab_split"), 2)
            weights()
            std(0)
            act.wait_ge(sem("normed"), 1)
            turn_nodes(1)
            for h in range(2):
                act.wait_ge(sem(f"gathered0_{h}"), 16 * HALF * RINGS)
                stage_idx(1, 0, h, F_SRC, True)
            spread_table(1)
            gather_loop(1)
            act.wait_ge(sem("parts_made1"), T // GT)
            act.dma_start(w_rel, W_rel.rearrange("r i o -> i r o")).then_inc(sem("rel_loaded"), 16)
            act.dma_start(b_rel_bc, b_rel.rearrange("r o -> (r o)").rearrange("(a c) -> a c", a=1).to_broadcast([P, R8 * D])).then_inc(sem("rel_loaded"), 16)
            std(1)
            act.wait_ge(sem("normed"), 2)
            turn_nodes(2)
            for h in range(2):
                act.wait_ge(sem(f"gathered1_{h}"), 16 * HALF * RINGS)
                stage_idx(2, 0, h, F_ROW, True)
            stage_all_idx(2, F_ROW)
            std(2)

            def rel_terms(n, p):
                act.wait_ge(sem("looked_up_g"), n + 1)
                act.activation(scaled[:, p, :, :].rearrange("p t c -> p (t c)"), bank(4 + p), ACT.Copy).then_inc(sem("rel_copied"), 1)

            def turn_message_hots(i, first):
                for p in range(2):
                    n = 2 * i + p
                    act.wait_ge(sem("transposed_g"), n + 1)
                    if not first:
                        act.wait_ge(sem("looked_up_g"), n - 1)
                    act.activation(ohT[:, p, 0, :], bank(p).bitcast(bf16)[:, 0:GT * P], ACT.Copy).then_inc(sem("ohT_g"), 1)
                    if not (first and p == 0):
                        if not first:
                            act.wait_ge(sem("msg_made"), n - 2)
                        rel_terms(n - 1, 1 - p)

            loop(act, T // GT // 2, turn_message_hots)
            rel_terms(T // GT - 1, 1)
            std(3)

        @block.tensor
        def _(pe):
            pe.wait_ge(sem("par_loaded"), 16 * (H + 7))
            pe.wait_ge(sem("masks"), 4)
            pe.transpose(bank(0, 0, D), w_nat[:, :], ident[:, :])
            pe.transpose(bank(0, D, 2 * D), wx[:, 1, 0:D], ident[:, :]).then_inc(sem("wT_made"), 1)
            pe.wait_ge(sem("aexp"), 1)
            pe.matmul(bank(1, 0, 2 * H), w_nat[:, :], aexp[:, 0:2, :].rearrange("p j h -> p (j h)"), start=True, stop=True)
            pe.wait_ge(sem("wpT"), 1)
            pe.matmul(bank(1, 32, 32 + 2 * H), wpT[:, :], aexp[:, 3:5, :].rearrange("p j h -> p (j h)"), start=True, stop=True)
            pe.matmul(bank(1, 64, 64 + H), we2[:, :], aexp[:, 2, :], start=True, stop=True).then_inc(sem("wa_made"), 1)
            pe.wait_ge(sem("dst_counted"), 1)
            pe.matmul(bank(7, 0, NB), tri[:, :], small[:, 0, 0:NB], start=True, stop=True)
            pe.matmul(bank(7, 32, 32 + NB), ones[:, :], small[:, 0, 0:NB], start=True, stop=True).then_inc(sem("dst_summed"), 1)

            pe.wait_ge(sem("wx_made"), 1)
            pe.wait_ge(sem("attr_cleared"), 1)

            def eatt(i, first):
                for h in range(2):
                    k = 2 * i + h
                    pe.wait_ge(sem(f"attr_loaded{h}"), attr_incs(i, h))
                    for q in range(2):
                        n = 2 * k + q
                        if not first or h:
                            pe.wait_ge(sem("attrT"), n - 1)
                        for j in range(4):
                            c = (4 * q + j) * 2 * KE
                            last = pe.transpose(bank(q, j * P, j * P + P), attr[:, h, c:c + 2 * KE], ident[:, :])
                        last.then_inc(sem("attr_transposed"), 1)
                    if not first:
                        pe.wait_ge(sem("rec_staged"), k - 1)
                    for q in range(2):
                        pe.wait_ge(sem("attrT"), 2 * k + q + 1)
                        for j in range(4):
                            c = (4 * q + j) * 2 * H
                            last = pe.matmul(bank(2 + h, c, c + 2 * H), scaled[:, q, j, :],
                                             wea2[:, :, :].rearrange("p a h -> p (a h)"), start=True, stop=True)
                        last.then_inc(sem("eatt_quad"), 1)

            def attr_incs(i, h):
                if not isinstance(i, int):
                    return 32 * i + 32
                return sum(32 if EREST > (2 * j + h) * HALF else 16 for j in range(i + 1))

            whole = EREST // (2 * HALF)
            eatt(0, True)
            with pe.Fori(1, whole) as i:
                eatt(i, False)
            for i in range(whole, RINGS):
                eatt(i, False)

            def turn_nodes(L, i, first):
                pe.wait_ge(sem(f"x_staged{L}"), i + 1)
                if not first:
                    pe.wait_ge(sem(f"xT{L}"), i)
                for j in range(XB):
                    last = pe.transpose(PS[:, j * P:j * P + P], x_stage[:, j * P:j * P + P], ident[:, :])
                last.then_inc(sem(f"x_turned{L}"), 1)
                pe.wait_ge(sem(f"xT{L}"), i + 1)

            def project(L):
                def body(i, first):
                    turn_nodes(L, i, first)
                    if not first:
                        pe.wait_ge(sem(f"projected{L}"), i)
                    for j in range(XB):
                        c = (j % 3) * PC
                        last = pe.matmul(bank(2 + j // 3, c, c + PC), xT[:, j * P:j * P + P], wx[:, L, :], start=True, stop=True)
                    last.then_inc(sem(f"proj_mm{L}"), 1)
                loop(pe, XI, body)

            def blocks_of(n, row):
                _, blocks = nc.values_load_multi_w_load_instructions(
                    row[0:1, bass.ds(n * GT, GT)], engines=[pe.engine], min_val=0, max_val=NB - 1,
                    skip_runtime_bounds_check_because="the ranking writes block numbers from 0 to NB - 1 only")
                return blocks

            def spread_table(L):
                pe.wait_ge(sem(f"projected{L}"), XI)
                for h in range(H):
                    last = pe.transpose(bank(6, h * P, h * P + P)[0:NB, :], tab_f[:, h, :], ident[:, :])
                last.then_inc(sem(f"tab_turned{L}"), 1)
                pe.wait_ge(sem(f"tab_T{L}"), 1)
                pe.wait_ge(sem(f"blk_hot{L}"), 1)
                for h in range(H):
                    for c in range(2):
                        pe.matmul(bank(2 * h + c, 0, MID), tab_T[0:NB, h * P:h * P + P], blk_hot[0:NB, c * MID:c * MID + MID],
                                  start=True, stop=True).then_inc(sem(f"tab_mm{L}"), 1)
                pe.wait_ge(sem("tab_split"), 1 + 2 * L)

            def look_up(out, h, q):
                for t in range(GT):
                    c = (q * GT + t) * P
                    for k in range(3):
                        last = pe.matmul(out[:, t * H:t * H + H], hotT[:, h, c:c + P], tab_h[:, h, q * GT + t, k, :],
                                         start=(k == 0), stop=(k == 2))
                return last

            def scores0():
                def look(n, h, q, i, early):
                    p = q % 2
                    pe.wait_ge(sem("hotT_made"), n + 1)
                    if q == 0:
                        pe.wait_ge(sem("tab_half_t0"), 2 * i + h + 1)
                    if not early:
                        pe.wait_ge(sem("scored0"), n - 1)
                    look_up(bank(2 + p, 0, GT * H), h, q).then_inc(sem("looked0"), 1)

                def spread(n, q, early):
                    p = q % 2
                    pe.wait_ge(sem("partsT"), n + 1)
                    for t in range(GT):
                        if t % 2 == 0 and not early:
                            pe.wait_ge(sem("maxed"), 2 * n - 1 + t // 2)
                        pe.matmul(bank(4 + t), hot4(q)[:, t * P:t * P + P], far_id[:, :, :].rearrange("p h c -> p (h c)"),
                                  start=True, stop=False, skip_group_check=True)
                        for h in range(H):
                            last = pe.matmul(bank(4 + t, h * P, h * P + P), pick[0:KP, t * H + h, :], apartT[0:KP, p, :],
                                             start=False, stop=True, skip_group_check=True)
                        if t % 2:
                            last.then_inc(sem("spread"), 1)

                def turn_parts(n, q):
                    pe.wait_ge(sem("scored0"), n + 1)
                    pe.transpose(bank(2 + q % 2, 64, 128).bitcast(bf16), apart[:, q % 2, :], ident_b[:, :]).then_inc(sem("parts_turned"), 1)

                def body(n, h, q, i, first):
                    p, start = q % 2, first and h == 0
                    pe.wait_ge(sem("hot_made"), n + 1)
                    if not (start and q < 2):
                        pe.wait_ge(sem("hotT_made"), n - 1)
                    for t in range(GT):
                        last = pe.transpose(bank(p).bitcast(bf16)[:, t * P:t * P + P], hot4(q)[:, t * P:t * P + P], ident_b[:, :])
                    last.then_inc(sem("turned"), 1)
                    h1, q1 = before(h, q)
                    h2, q2 = before(h1, q1)
                    if not (start and q == 0):
                        look(n - 1, h1, q1, i, start and q < 3)
                    if not (start and q < 2):
                        spread(n - 2, q2, start and q < 3)
                    if not (start and q == 0):
                        turn_parts(n - 1, q1)

                ring_steps(pe, body)
                look(LASTG, 1, GPH - 1, RINGS - 1, False)
                spread(LASTG - 1, GPH - 2, False)
                turn_parts(LASTG, GPH - 1)
                spread(LASTG, GPH - 1, False)

            def clear_sums():
                for k in range(ACC_BANKS):
                    pe.matmul(bank(k), zeros[:, 0:P], zeros[:, :], start=True, stop=True)

            def weighted_sums(L):
                ns = 2 * H if L == 0 else H

                def add(n, q):
                    pe.wait_ge(sem(f"parts_made{L}"), n + 1)
                    blocks = blocks_of(n, blk_dst)
                    for t in range(GT):
                        hot = hot4(q)[:, t * P:t * P + P]
                        for k in range(3):
                            pe.matmul(PS[:, bass.ds(blocks[t] * D, D)], hot, parts[q][:, k, t, 0:D],
                                      start=False, stop=True, skip_group_check=True)
                        for k in range(3):
                            m = ns + 1 if L == 0 and k == 0 else ns
                            last = pe.matmul(PS[:, bass.ds(blocks[t] * NS + SUM0, m)], hot, parts[q][:, k, t, D:D + m],
                                             start=False, stop=True, skip_group_check=True)
                    last.then_inc(sem(f"acc{L}"), 1)

                def body(n, h, q, i, first):
                    start = first and h == 0
                    if L == 0:
                        if q == 0:
                            pe.wait_ge(sem(f"hotT_loaded0_{h}"), 16 * i + 16)
                            pe.wait_ge(sem("tab_half_m"), 2 * i + h + 1)
                        if not (start and q == 0):
                            pe.wait_ge(sem("weights_made0"), n)
                        look_up(bank(7, 0, GT * H), h, q).then_inc(sem("looked_m"), 1)
                    if not start:
                        add(n - GPH, q)

                def half_body(i, first, last=False):
                    for h in range(2):
                        m, start = 2 * i + h, first and h == 0
                        n = GPH * m
                        pe.wait_ge(sem("lane_max"), m + 1)
                        pe.matmul(bank(7, P, 2 * P)[0:1, :], small[:, 5, 0:1], ident[:, :], start=True, stop=True).then_inc(sem("lane_max_turned"), 1)
                        pe.wait_ge(sem("one_max"), m + 1)
                        pe.matmul(bank(7, 3 * P, 3 * P + 1), ones[0:1, :], small[0:1, 5, 1:2], start=True, stop=True).then_inc(sem("max_spread"), 1)
                        if not start:
                            add(n - 1, 3)
                        if h == 0:
                            look_half(i, 1)
                        elif not last:
                            look_half(i + 1, 0)
                        if not start:
                            pe.wait_ge(sem("rescaled_v"), m)
                            pe.wait_ge(sem("rescaled_a"), m)
                        for q in range(3):
                            add(n + q, q)

                def look_half(i, h):
                    pe.wait_ge(sem(f"hotT_loaded1_{h}"), 16 * i + 16)
                    pe.wait_ge(sem("tab_half_t1"), 2 * i + h + 1)
                    if not isinstance(i, int) or i or h:
                        pe.wait_ge(sem("max_ready"), 2 * i + h)
                    for q in range(GPH):
                        look_up(bank(7, q * GT * H, (q + 1) * GT * H), h, q).then_inc(sem("looked1"), 1)

                if L == 1:
                    look_half(0, 0)
                    half_body(0, True)
                    half_body(1, False)
                    with pe.Fori(2, RINGS - 1) as i:
                        half_body(i, False)
                    half_body(RINGS - 1, False, True)
                    add(LASTG, 3)
                    return
                ring_steps(pe, body)
                for q in range(GPH):
                    add(T // GT - GPH + q, q)

            def accumulate(L, row):
                def body(n, h, q, i, first):
                    if q == 0 and L == 2:
                        pe.wait_ge(sem(f"gathered{L}_{h}"), 16 * HALF * i + 16 * HALF)
                    pe.wait_ge(sem(f"weighted{L}"), n + 1)
                    blocks = blocks_of(n, row)
                    for t in range(GT):
                        last = pe.matmul(PS[:, bass.ds(blocks[t] * D, D)], ohf[:, q % 2, t, :], ring[:, h, q * GT + t, 0:D],
                                         start=False, stop=True, skip_group_check=True)
                    last.then_inc(sem(f"acc{L}"), 1)

                if L == 3:
                    ring_steps(pe, body)
                    return

                def step(i, first=False):
                    for h in range(2):
                        for q in range(GPH):
                            body(2 * GPH * i + GPH * h + q, h, q, i, first)

                step(0)
                step(1)
                with pe.Fori(2, SUM_AT) as i:
                    step(i)
                pe.wait_ge(sem("src_counted"), 1)
                pe.matmul(bank(7, 0, NB), tri[:, :], small[:, 0, 0:NB], start=True, stop=True)
                pe.matmul(bank(7, 32, 32 + NB), ones[:, :], small[:, 0, 0:NB], start=True, stop=True).then_inc(sem("src_summed"), 1)
                with pe.Fori(SUM_AT, RINGS) as i:
                    step(i)

            pe.wait_ge(sem("rec_staged"), 2 * RINGS)
            pe.wait_ge(sem("attrT"), 4 * RINGS)
            pe.wait_ge(sem("x_loaded"), 32)
            project(0)
            spread_table(0)
            scores0()
            pe.wait_ge(sem("maxed"), 2 * (T // GT))
            pe.wait_ge(sem("blk_loaded"), 16)
            clear_sums()
            weighted_sums(0)
            pe.wait_ge(sem("normed"), 1)
            project(1)
            spread_table(1)
            clear_sums()
            weighted_sums(1)
            pe.wait_ge(sem("normed"), 2)
            pe.wait_ge(sem("rel_loaded"), 32)

            def relate(i, first):
                turn_nodes(2, i, first)
                for j in range(XB):
                    n = XB * i + j
                    if not first or j > 2:
                        pe.wait_ge(sem("rel_made"), n - 1)
                    for k in range(2):
                        last = pe.matmul(bank(2 + 2 * (j % 3) + k), xT[:, j * P:j * P + P],
                                         w_rel.rearrange("p r c -> p (r c)")[:, k * BK:(k + 1) * BK], start=True, stop=True)
                    last.then_inc(sem("rel_mm"), 1)

            loop(pe, XI, relate)
            pe.wait_ge(sem("rel_made"), NB)
            pe.wait_ge(sem("xT2"), XI)
            clear_sums()
            accumulate(2, blk_dst)
            pe.wait_ge(sem("x_split"), 1)

            def message_terms(n, h, q, i, early):
                p = q % 2
                pe.wait_ge(sem("ohT_g"), n + 1)
                if q == 0:
                    pe.wait_ge(sem(f"hotT_loaded3_{h}"), 16 * i + 16)
                if not early:
                    pe.wait_ge(sem("rel_copied"), n - 1)
                    pe.wait_ge(sem("msg_made"), n - 1)
                blocks = blocks_of(n, blk_dst)
                for t in range(GT):
                    c = (q * GT + t) * P
                    for k in range(3):
                        pe.matmul(bank(2 + p, t * P, t * P + P), hotT[:, h, c:c + P],
                                  xs3[:, k, bass.ds(blocks[t] * D, D)], start=(k == 0), stop=(k == 2))
                    for k in range(3):
                        last = pe.matmul(bank(4 + p, t * P, t * P + P), ohT[:, p, 0, t * P:t * P + P], w24s[:, k, :],
                                         start=(k == 0), stop=(k == 2))
                last.then_inc(sem("looked_up_g"), 1)

            def message_body(n, h, q, i, first):
                p, start = q % 2, first and h == 0
                pe.wait_ge(sem("one_hot_g"), n + 1)
                if not (start and q < 2):
                    pe.wait_ge(sem("ohT_g"), n - 1)
                for t in range(GT):
                    last = pe.transpose(bank(p).bitcast(bf16)[:, t * P:t * P + P], hot4(q)[:, t * P:t * P + P], ident_b[:, :])
                last.then_inc(sem("transposed_g"), 1)
                if not (start and q == 0):
                    message_terms(n - 1, *before(h, q), i, start and q < 3)

            ring_steps(pe, message_body)
            message_terms(LASTG, 1, GPH - 1, RINGS - 1, False)
            pe.wait_ge(sem("msg_made"), T // GT)
            pe.wait_ge(sem("blk_loaded"), 32)
            clear_sums()
            accumulate(3, blk_src)


KIND = "Internal"

_INS = ['x', 'src', 'dst', 'edge_attr_64', 'edge_type_24', 'edge_type_8', 'edge_weight1', 'L0_gnn_W_node',
        'L0_gnn_W_edge', 'L0_gnn_a', 'L1_gnn_W_proj', 'L1_gnn_a_src', 'L1_gnn_a_tgt', 'L1_gnn_bias', 'L2_gnn_W',
        'L2_gnn_b', 'L3_gnn_weight']


def kernel(**inputs):
    import numpy as _np
    import concourse.bacc as _bacc
    from concourse import mybir as _mybir
    from concourse.bass_utils import run_bass_kernel_spmd as _run

    nc = _bacc.Bacc("TRN2", target_bir_lowering=False, num_devices=1)
    arrays, args = {}, []
    for name in _INS:
        a = _np.ascontiguousarray(inputs[name])
        arrays[f"in_{name}_dram"] = a
        args.append(nc.dram_tensor(f"in_{name}_dram", a.shape, _mybir.dt.from_np(a.dtype), kind="ExternalInput").ap())
    args.append(nc.dram_tensor("out_dram", (3125, 128), _mybir.dt.float32, kind="ExternalOutput").ap())
    gnn_resnorm_kernel(nc, *args)
    r = _run(nc, [arrays], core_ids=[0])
    return r.results[0]["out_dram"]
```
